# Optimizing a Trainium2 kernel written in Bass

```python
import numpy as np
import jax
import jax.numpy as jnp

def _softmax(x, axis=-1):
    return jax.nn.softmax(x, axis=axis)

def _gelu(x):
    return jax.nn.gelu(x, approximate=True)

def _silu(x):
    return jax.nn.silu(x)

def _sigmoid(x):
    return jax.nn.sigmoid(x)

def _layernorm(x, axis=-1, eps=1e-05):
    m = jnp.mean(x, axis=axis, keepdims=True)
    v = jnp.var(x, axis=axis, keepdims=True)
    return (x - m) / jnp.sqrt(v + eps)

def _scatter_add(tgt, idx, src, axis=0):
    return tgt.at[idx].add(src)

def _segment_sum(src, seg, n):
    return jax.ops.segment_sum(src, seg, n)
kernel_name = 'mk_lm_tower_d1_tok_ids512_r4_3669be'

def setup_inputs(seed: int=0):
    np.random.seed(seed)
    _w = jnp.asarray

    def _rec_inputs():
        import jax
        import jax.numpy as jnp
        _rk = jax.random.key(seed)
        x = jax.random.randint(jax.random.fold_in(_rk, 1), (8, 512), 0, 125, jnp.int32)
        return x
    x = _rec_inputs()

    def _L0_tok_setup():
        import jax, jax.numpy as jnp
        import numpy as np
        QMAX = 127.0
        CTX = 2

        def fake_quant(w):
            scale = jnp.max(jnp.abs(w)) / QMAX
            wq = jnp.round(w / scale) * scale
            return w + jax.lax.stop_gradient(wq - w)
        key = jax.random.key(seed)
        k1, k2, k3 = jax.random.split(key, 3)
        y = jax.random.randint(k1, (64, 512), 0, 125, dtype=jnp.int64)
        emb_weight = jax.random.normal(k2, (125, 128), dtype=jnp.float32)
        conv_weight = jax.random.normal(k3, (128, 1, 2), dtype=jnp.float32)
        return {'y': y, 'emb_weight': emb_weight, 'conv_weight': conv_weight}
    _L0_tok_all = _L0_tok_setup()
    _L0_tok_in = {k: v for k, v in _L0_tok_all.items() if k in ('emb_weight', 'conv_weight')}
    del _L0_tok_all

    def _L0_attn_setup():
        import jax, jax.numpy as jnp
        import numpy as np
        PI = np.float32(np.pi)

        def goom_log(x):
            return jax.lax.complex(jnp.log(jnp.abs(x)).astype(jnp.float32), jnp.where(x < 0, PI, np.float32(0.0)))

        def log_matmul_exp(LA, LB):
            c1 = jnp.max(LA.real, axis=-1, keepdims=True)
            c2 = jnp.max(LB.real, axis=-2, keepdims=True)
            c1 = jnp.where(jnp.isfinite(c1), c1, np.float32(0.0))
            c2 = jnp.where(jnp.isfinite(c2), c2, np.float32(0.0))
            P = jnp.matmul(jnp.exp(LA - c1), jnp.exp(LB - c2))
            return jnp.log(P) + c1 + c2
        key = jax.random.key(seed)
        ks = jax.random.split(key, 6)
        d_inp, d_out, n_hid, d_hid = (128, 128, 4, 64)
        Bsz, L = (8, 256)
        u = jax.random.normal(ks[0], (Bsz, L, d_inp), dtype=jnp.float32)
        init_states = jax.random.uniform(ks[1], (n_hid, d_hid), minval=-0.1, maxval=0.1, dtype=jnp.float32)
        Q, _ = jnp.linalg.qr(jax.random.normal(ks[2], (d_hid, d_hid), dtype=jnp.float32))
        A = np.float32(0.99) * Q
        B = jax.random.uniform(ks[3], (d_inp, n_hid * d_hid), minval=-1.0, maxval=1.0, dtype=jnp.float32) / np.float32(np.sqrt(d_inp))
        C = jax.random.uniform(ks[4], (n_hid * d_hid, d_out), minval=-1.0, maxval=1.0, dtype=jnp.float32) / np.float32(np.sqrt(n_hid * d_hid))
        D = jax.random.uniform(ks[5], (d_inp, d_out), minval=-1.0, maxval=1.0, dtype=jnp.float32) / np.float32(np.sqrt(d_inp))
        return {'u': u, 'init_states': init_states, 'A': A, 'B': B, 'C': C, 'D': D}
    _L0_attn_all = _L0_attn_setup()
    _L0_attn_in = {k: v for k, v in _L0_attn_all.items() if k in ('init_states', 'A', 'B', 'C', 'D')}
    del _L0_attn_all

    def _L0_ffn_setup():
        import jax, jax.numpy as jnp
        import numpy as np
        MICRO_BATCHES = 2
        TOP_K = 2
        D = 128
        E = 8
        B, S = (8, 2048)
        key = jax.random.key(seed)
        ks = jax.random.split(key, 12)
        s = 0.02
        return {'x': jax.random.normal(ks[0], (B, S, D), dtype=jnp.float32), 'ln_g': jnp.ones((D,), jnp.float32), 'ln_b': jnp.zeros((D,), jnp.float32), 'attn_w': jax.random.normal(ks[1], (D, D), jnp.float32) * s, 'attn_b': jnp.zeros((D,), jnp.float32), 'gate_w': jax.random.normal(ks[2], (E, D), jnp.float32) * s, 'fc1_w': jax.random.normal(ks[3], (E, 4 * D, D), jnp.float32) * s, 'fc1_b': jnp.zeros((E, 4 * D), jnp.float32), 'fc2_w': jax.random.normal(ks[4], (E, D, 4 * D), jnp.float32) * s, 'fc2_b': jnp.zeros((E, D), jnp.float32), 'next_w': jax.random.normal(ks[5], (D, D), jnp.float32) * s, 'next_b': jnp.zeros((D,), jnp.float32)}
    _L0_ffn_all = _L0_ffn_setup()
    _L0_ffn_in = {k: v for k, v in _L0_ffn_all.items() if k in ('ln_g', 'ln_b', 'attn_w', 'attn_b', 'gate_w', 'fc1_w', 'fc1_b', 'fc2_w', 'fc2_b', 'next_w', 'next_b')}
    del _L0_ffn_all
    return {'x': x, 'L0_tok_emb_weight': _L0_tok_in['emb_weight'], 'L0_tok_conv_weight': _L0_tok_in['conv_weight'], 'L0_attn_init_states': _L0_attn_in['init_states'], 'L0_attn_A': _L0_attn_in['A'], 'L0_attn_B': _L0_attn_in['B'], 'L0_attn_C': _L0_attn_in['C'], 'L0_attn_D': _L0_attn_in['D'], 'L0_ffn_ln_g': _L0_ffn_in['ln_g'], 'L0_ffn_ln_b': _L0_ffn_in['ln_b'], 'L0_ffn_attn_w': _L0_ffn_in['attn_w'], 'L0_ffn_attn_b': _L0_ffn_in['attn_b'], 'L0_ffn_gate_w': _L0_ffn_in['gate_w'], 'L0_ffn_fc1_w': _L0_ffn_in['fc1_w'], 'L0_ffn_fc1_b': _L0_ffn_in['fc1_b'], 'L0_ffn_fc2_w': _L0_ffn_in['fc2_w'], 'L0_ffn_fc2_b': _L0_ffn_in['fc2_b'], 'L0_ffn_next_w': _L0_ffn_in['next_w'], 'L0_ffn_next_b': _L0_ffn_in['next_b']}

def reference(x, L0_tok_emb_weight, L0_tok_conv_weight, L0_attn_init_states, L0_attn_A, L0_attn_B, L0_attn_C, L0_attn_D, L0_ffn_ln_g, L0_ffn_ln_b, L0_ffn_attn_w, L0_ffn_attn_b, L0_ffn_gate_w, L0_ffn_fc1_w, L0_ffn_fc1_b, L0_ffn_fc2_w, L0_ffn_fc2_b, L0_ffn_next_w, L0_ffn_next_b):
    import jax
    import jax.numpy as jnp

    def _L0_tok_ref(y, emb_weight, conv_weight):
        import jax, jax.numpy as jnp
        import numpy as np
        QMAX = 127.0
        CTX = 2

        def fake_quant(w):
            scale = jnp.max(jnp.abs(w)) / QMAX
            wq = jnp.round(w / scale) * scale
            return w + jax.lax.stop_gradient(wq - w)
        w_emb = fake_quant(emb_weight)
        e = w_emb[jnp.clip(y, 0)]
        e = e * (y >= 0)[..., None].astype(e.dtype)
        x = jnp.pad(e, ((0, 0), (CTX - 1, 0), (0, 0)))
        D = conv_weight.shape[0]
        w = fake_quant(conv_weight).transpose(2, 1, 0)
        out = jax.lax.conv_general_dilated(x, w, window_strides=(1,), padding='VALID', feature_group_count=D, dimension_numbers=('NWC', 'WIO', 'NWC'))
        return jax.nn.relu(out)

    def _L0_attn_ref(u, init_states, A, B, C, D):
        import jax, jax.numpy as jnp
        import numpy as np
        PI = np.float32(np.pi)

        def goom_log(x):
            return jax.lax.complex(jnp.log(jnp.abs(x)).astype(jnp.float32), jnp.where(x < 0, PI, np.float32(0.0)))

        def log_matmul_exp(LA, LB):
            c1 = jnp.max(LA.real, axis=-1, keepdims=True)
            c2 = jnp.max(LB.real, axis=-2, keepdims=True)
            c1 = jnp.where(jnp.isfinite(c1), c1, np.float32(0.0))
            c2 = jnp.where(jnp.isfinite(c2), c2, np.float32(0.0))
            P = jnp.matmul(jnp.exp(LA - c1), jnp.exp(LB - c2))
            return jnp.log(P) + c1 + c2
        Bsz, L, d_inp = u.shape
        n, d = init_states.shape
        Bu = jnp.matmul(u, B).reshape(Bsz, L, n, d)
        A_b = jnp.broadcast_to(A, (Bsz, L, d, d))
        log_el = goom_log(jnp.concatenate([A_b, Bu], axis=-2))
        L0I = goom_log(jnp.concatenate([jnp.zeros((d, n), jnp.float32), jnp.eye(n, dtype=jnp.float32)], axis=0))

        def combine(e1, e2):
            aug = jnp.concatenate([e1, jnp.broadcast_to(L0I, e1.shape[:-1] + (n,))], axis=-1)
            return log_matmul_exp(aug, e2)
        log_cum = jax.lax.associative_scan(combine, log_el, axis=1)
        log_x0 = goom_log(init_states)
        log_I = goom_log(jnp.eye(n, dtype=jnp.float32))
        log_x0_I = jnp.concatenate([log_x0, log_I], axis=-1)
        log_x = log_matmul_exp(log_x0_I, log_cum)
        c = jax.lax.stop_gradient(jnp.max(log_x.real, axis=-1, keepdims=True))
        x = jnp.exp(log_x - c + 2).real.reshape(Bsz, L, n * d)
        y = jnp.matmul(x, C) + jnp.matmul(u, D)
        return y

    def _L0_ffn_ref(x, ln_g, ln_b, attn_w, attn_b, gate_w, fc1_w, fc1_b, fc2_w, fc2_b, next_w, next_b):
        import jax, jax.numpy as jnp
        import numpy as np
        MICRO_BATCHES = 2
        TOP_K = 2
        D = 128
        E = 8
        B, S = (8, 2048)
        b, s, d = x.shape
        xf = x.reshape(b * s, d)
        mu = jnp.mean(xf, axis=-1, keepdims=True)
        var = jnp.var(xf, axis=-1, keepdims=True)
        normed = (xf - mu) / jnp.sqrt(var + 1e-05) * ln_g + ln_b
        x_attn = normed @ attn_w.T + attn_b + xf
        logits = x_attn @ gate_w.T
        _scores, _indices = jax.lax.top_k(logits, TOP_K)
        e = fc1_w.shape[0]
        t = b * s // (MICRO_BATCHES * e)
        tok = x_attn.reshape(MICRO_BATCHES, e, t, d)
        h = jnp.einsum('meti,ehi->meth', tok, fc1_w) + fc1_b[None, :, None, :]
        h = jax.nn.gelu(h, approximate=False)
        y = jnp.einsum('meth,edh->metd', h, fc2_w) + fc2_b[None, :, None, :]
        yf = y.reshape(b * s, d)
        out = jax.nn.gelu(yf @ next_w.T + next_b, approximate=False)
        return out.reshape(b, s, d)
    h = _L0_tok_ref(x, L0_tok_emb_weight, L0_tok_conv_weight)
    h = h + _L0_attn_ref(_layernorm(h, axis=-1), L0_attn_init_states, L0_attn_A, L0_attn_B, L0_attn_C, L0_attn_D)
    h = h + _L0_ffn_ref(_layernorm(h, axis=-1), L0_ffn_ln_g, L0_ffn_ln_b, L0_ffn_attn_w, L0_ffn_attn_b, L0_ffn_gate_w, L0_ffn_fc1_w, L0_ffn_fc1_b, L0_ffn_fc2_w, L0_ffn_fc2_b, L0_ffn_next_w, L0_ffn_next_b)
    return h

_drawn_inputs = setup_inputs


def setup_inputs(seed=0):
    import zlib

    import numpy as np

    out = dict(_drawn_inputs(seed))
    spreads = {'L0_ffn_ln_g': (1.0, 0.6),
     'L0_ffn_ln_b': (0.0, 0.8),
     'L0_ffn_attn_b': (0.0, 0.8),
     'L0_ffn_fc1_b': (0.0, 0.8),
     'L0_ffn_fc2_b': (0.0, 0.8),
     'L0_ffn_next_b': (0.0, 2.0)}
    factors = {'L0_attn_init_states': 6.796,
     'L0_ffn_attn_w': 8.0,
     'L0_ffn_fc1_w': 8.0,
     'L0_ffn_fc2_w': 8.0,
     'L0_ffn_next_w': 8.0}
    for name, (base, spread) in spreads.items():
        noise = np.random.default_rng([zlib.crc32(name.encode()), seed]).standard_normal(out[name].shape)
        drawn = base * np.exp(spread * noise) if base else spread * noise
        out[name] = jnp.asarray(drawn.astype(out[name].dtype))
    for name, factor in factors.items():
        out[name] = (out[name] * factor).astype(out[name].dtype)
    return out
```

```python
from contextlib import ExitStack

import concourse.bass as bass
import numpy as np
from concourse import mybir

ALU = mybir.AluOpType
ACT = mybir.ActivationFunctionType
AX = mybir.AxisListType
F32 = mybir.dt.float32
BF16 = mybir.dt.bfloat16
I32 = mybir.dt.int32

P = 128
NB = 8
L = 512
T = 16
NCH = L // T
NG = 2
GB = NB // NG
VOC = 125
NH, DH = 4, 64
NP = NH * DH // P
CH = 128
NE, HID = 8, 512
HC = HID // P
TQ = P // NCH
NQ = T // TQ
EXT = T + 1
HALF = L // 2
QMAX = 127.0
EPS = 1e-5
ROUND = 12582912.0
E2 = float(np.exp(np.float32(2.0)))
NS = 3
LEVELS = NCH.bit_length() - 1

PA_COLS = dict(a=P, at=P, ident=P, b=NP * P, iota=1, init=NP, ln_g=1, ln_b=1, attn_b=1, next_b=1,
               fc1_b=NE * HC, fc2_b=NE)
PB_COLS = dict(nw=CH, c=NP * CH, d=CH, attn=CH)


def spans(cols):
    out, at = {}, 0
    for name, n in cols.items():
        out[name] = slice(at, at + n)
        at += n
    return out, at


PA, PA_N = spans(PA_COLS)
PB, PB_N = spans(PB_COLS)


def build(nc, ids, emb, conv, pack_a, pack_b, sel, ident_b, fc1, fc2, out):
    with ExitStack() as ctx:
        def sb(name, shape, dt=F32):
            return ctx.enter_context(nc.sbuf_tensor(name, shape, dt))

        def sem(name):
            return ctx.enter_context(nc.semaphore(name))

        ids_i = sb("ids_i", [2 * NB, EXT * NCH // 2], I32)
        ids_b = sb("ids_b", [2 * NB, EXT * NCH // 2], BF16)
        rowsel = sb("rowsel", [2 * NB, 2 * NB, P], BF16)
        emb_w = sb("emb_w", [VOC, CH])
        conv_w = sb("conv_w", [P, 2 * CH])
        pa = sb("pa", [P, PA_N])
        pb = sb("pb", [P, PB_N])
        sel_b = sb("sel_b", [NS * NQ * NH, NQ * NP * P], BF16)
        idn_b = sb("idn_b", [P, P], BF16)
        fc1_w = sb("fc1_w", [P, NE * HID])
        fc2_w = sb("fc2_w", [P, NE * HID])
        out_w = sb("out_w", [P, NE, HC, CH])
        ones1 = sb("ones1", [1, P])
        neg_half = sb("neg_half", [P, NQ])
        inv_e = sb("inv_e", [P, 1])
        inv_c = sb("inv_c", [P, 1])
        amax_e = sb("amax_e", [VOC, 1])
        amax_row = sb("amax_row", [1, 1])
        scale_e = sb("scale_e", [P, 1])
        scale_c = sb("scale_c", [P, 1])
        scale_h = sb("scale_h", [P, 1])
        q_e = sb("q_e", [VOC, CH])
        q_c = sb("q_c", [P, 2 * CH])
        prod = sb("prod", [VOC, 2, CH])
        tab = sb("tab", [VOC, 2, 2, CH], BF16)
        onehot = sb("onehot", [VOC, 2, EXT * NCH], BF16)
        h = sb("h", [P, NB, NQ * CH])
        st1 = sb("st1", [P, 2, NQ, 6])
        mv1 = sb("mv1", [P, NB, NQ, 2])
        rstd1 = sb("rstd1", [P, NB, NQ])
        var_eps = sb("var_eps", [P, NQ])
        u = sb("u", [P, 2, NQ * CH])
        uT = sb("uT", [P, NB, T, NCH])
        pw = sb("pw", [P, T + 1, P])
        pw_t = sb("pw_t", [P, T + 1, P])
        pk = sb("pk", [P, LEVELS, P])
        pk_t = sb("pk_t", [P, LEVELS, P])
        attn_g = sb("attn_g", [P, CH])
        attn_c = sb("attn_c", [P, 1])
        out_c = sb("out_c", [P, NE])
        X = sb("X", [P, NG, NP * GB, T, NCH])
        E = sb("E", [P, NG, NP * GB, NCH])
        amax = sb("amax", [P, 2, NQ, NH])
        rcp = sb("rcp", [P, 2, NQ * NH])
        r_f = sb("r_f", [P, NQ * NH])
        r_d = sb("r_d", [P, 2, NQ * NH])
        r_s = sb("r_s", [P, 2, NS, NQ * NH], BF16)
        r_T = sb("r_T", [NS * NQ * NH, 2, P], BF16)
        xh = sb("xh", [P, 2, NP, L])
        st2 = sb("st2", [P, 2, NQ, 6])
        mv2 = sb("mv2", [P, NB, NQ, 2])
        rstd2 = sb("rstd2", [P, NB, NQ])
        rstd3 = sb("rstd3", [P, NB, NQ])
        sq = sb("sq", [P, 4, NQ])
        xp = sb("xp", [P, 2, NQ * CH])
        xpT = sb("xpT", [P, 2, L])
        xa = sb("xa", [P, 2, NQ * CH])
        xaT = sb("xaT", [P, 2, 2, HALF])
        hid = sb("hid", [P, 2, HC, HALF])
        gel = sb("gel", [P, 2, L])
        res = sb("res", [P, 2, L])
        bank = [ctx.enter_context(nc.psum_tensor(f"bank{n}", [P, 512], F32)) for n in range(8)]
        bank_rt = bank[4][0:NS * NQ * NH, 0:P // 2].bitcast(BF16)

        ident = pa[:, PA["ident"]]

        ld_ids, ld_emb, ld_pa, ld_pb = sem("ld_ids"), sem("ld_emb"), sem("ld_pa"), sem("ld_pb")
        ld_const, ld_fc1, ld_fc2 = sem("ld_const"), sem("ld_fc1"), sem("ld_fc2")
        pool_const = sem("pool_const")
        pool_link, dve_link = sem("pool_link"), sem("dve_link")
        ids_ready, amax_e_ready, amax_row_ready, tab_ready = (
            sem("ids_ready"), sem("amax_e_ready"), sem("amax_row_ready"), sem("tab_ready"))
        attn_g_ready = sem("attn_g_ready")
        amax_t_done, amax_bc_done = sem("amax_t_done"), sem("amax_bc_done")
        idb_done, oh_ready, gat_done, h_ready = sem("idb_done"), sem("oh_ready"), sem("gat_done"), sem("h_ready")
        st1_ready, mv1_ready, rstd1_ready, u_ready = (
            sem("st1_ready"), sem("mv1_ready"), sem("rstd1_ready"), sem("u_ready"))
        u_t_done, uT_ready = sem("u_t_done"), sem("uT_ready")
        prep_done, prep_ready = sem("prep_done"), sem("prep_ready")
        step_done, x_ready = [sem(f"step_done{g}") for g in range(NG)], [sem(f"x_ready{g}") for g in range(NG)]
        init_ready, ends_ready = sem("init_ready"), [sem(f"ends_ready{g}") for g in range(NG)]
        ks_done, ks_ready = [sem(f"ks_done{g}") for g in range(NG)], [sem(f"ks_ready{g}") for g in range(NG)]
        p2_done, x2_ready = [sem(f"p2_done{g}") for g in range(NG)], [sem(f"x2_ready{g}") for g in range(NG)]
        xt_done, amax_ready, rcp_ready, rs_ready = (
            sem("xt_done"), sem("amax_ready"), sem("rcp_ready"), sem("rs_ready"))
        rt_done, rT_ready, R_done, xh_ready = sem("rt_done"), sem("rT_ready"), sem("R_done"), sem("xh_ready")
        y_done, h2_ready, st2_ready, mv2_ready = sem("y_done"), sem("h2_ready"), sem("st2_ready"), sem("mv2_ready")
        rstd2_ready, rstd3_ready, xp_ready = sem("rstd2_ready"), sem("rstd3_ready"), sem("xp_ready")
        xp_t_done, xpT_ready, attn_done, xa_ready = (
            sem("xp_t_done"), sem("xpT_ready"), sem("attn_done"), sem("xa_ready"))
        xa_t_done, xaT_ready = sem("xa_t_done"), sem("xaT_ready")
        fc1_done, hid_ready, o_done, gel_ready = sem("fc1_done"), sem("hid_ready"), sem("o_done"), sem("gel_ready")
        h2_t_done, res_ready = sem("h2_t_done"), sem("res_ready")
        stored = [sem("stored0"), sem("stored1")]

        def powers(n0, n1):
            return pw[:, n0:n1 + 1, :].rearrange("p n m -> p (n m)")

        a1, a1t = pa[:, PA["a"]], pa[:, PA["at"]]
        prep = [
            (powers(2, 2), a1t, a1, 0), (pw_t[:, 2, :], a1, a1t, 0),
            (pw[:, 3, :], pw_t[:, 2, :], a1, 2), (pw[:, 4, :], pw_t[:, 2, :], pw[:, 2, :], 2),
            (pw_t[:, 4, :], pw[:, 2, :], pw_t[:, 2, :], 2),
            (powers(5, 8), pw_t[:, 4, :], powers(1, 4), 5), (pw_t[:, 8, :], pw[:, 4, :], pw_t[:, 4, :], 5),
            (powers(9, 12), pw_t[:, 8, :], powers(1, 4), 7), (powers(13, 16), pw_t[:, 8, :], powers(5, 8), 7),
            (pw_t[:, T, :], pw[:, 8, :], pw_t[:, 8, :], 7),
        ]
        prev, prev_t = pw[:, T, :], pw_t[:, T, :]
        for lv in range(1, LEVELS):
            need = len(prep)
            prep.append((pk[:, lv, :], prev_t, prev, need))
            if lv < LEVELS - 1:
                prep.append((pk_t[:, lv, :], prev, prev_t, need))
            prev, prev_t = pk[:, lv, :], pk_t[:, lv, :]
        N_POW = len(prep)
        N_PREP = N_POW + NE + 1

        def step_of(n):
            return pw[:, T, :] if n == 0 else pk[:, n, :]

        def ks_src(g, lv):
            return E[:, g, :, 0:NCH - 2 ** lv]

        def ks_dst(g, lv):
            return E[:, g, :, 2 ** lv:NCH]

        def ks_bank(g, lv):
            n = NP * GB * (NCH - 2 ** lv)
            return bank[2 + g][:, 0:n].rearrange("p (a k) -> p a k", a=NP * GB)

        def x_step(g, i):
            return X[:, g, :, i, :]

        def expert(b, half):
            return (2 * b + half) % NE

        G0_FRONT = 12
        KS0_AT = 4
        P2_AT = KS0_AT + LEVELS

        with nc.Block() as block:

            @block.sync
            def _(sp):
                sp.dma_start(ids_i[:], ids).then_inc(ld_ids, 16)
                sp.dma_start(emb_w[:], emb).then_inc(ld_emb, 16)
                sp.dma_start(pa[:], pack_a).then_inc(ld_pa, 16)
                sp.dma_start(pw[:, 1, :], pack_a[:, PA["a"]]).then_inc(ld_pa, 16)
                sp.dma_start(pb[:], pack_b).then_inc(ld_pb, 16)
                sp.dma_start(fc2_w[:].rearrange("p (e m) -> p e m", e=NE), fc2).then_inc(ld_fc2, 16)
                sp.dma_start(fc1_w[:], fc1).then_inc(ld_fc1, 16)
                for b in range(NB):
                    sp.wait_ge(res_ready, b + 1)
                    sp.dma_start(out[b], res[:, b % 2, :]).then_inc(stored[b % 2], 16)
                for s in range(2):
                    sp.wait_ge(stored[s], 16 * (NB // 2))

            @block.gpsimd
            def _(pool):
                nc.gpsimd.memset(rowsel[:], 0.0).then_inc(pool_link, 1)
                nc.gpsimd.memset(ones1[:], 1.0).then_inc(pool_const, 1)
                nc.gpsimd.memset(neg_half[:], -0.5).then_inc(pool_const, 1)
                pool.wait_ge(pool_link, 1)
                nc.gpsimd.affine_select(out=rowsel[:], in_=rowsel[:], compare_op=ALU.not_equal, fill=1.0, base=0,
                                        pattern=[[-1, 2 * NB], [0, P]], channel_multiplier=1).then_inc(pool_const, 1)
                link = [1]

                def chained(ins):
                    link[0] += 1
                    ins.then_inc(pool_link, 1)
                    pool.wait_ge(pool_link, link[0])

                pool.wait_ge(pool_const, 3)
                for b in range(NB):
                    pool.wait_ge(mv1_ready, b + 1)
                    chained(nc.gpsimd.tensor_scalar(var_eps[:], mv1[:, b, :, 1], EPS, None, ALU.add))
                    nc.gpsimd.tensor_tensor(rstd1[:, b, :], var_eps[:], neg_half[:], ALU.pow).then_inc(rstd1_ready, 1)

                pool.wait_ge(ld_pa, 32)
                for g in range(NG):
                    for a in range(NP):
                        last = nc.gpsimd.tensor_copy(E[:, g, a * GB:(a + 1) * GB, 0],
                                                     pa[:, PA["init"]][:, a:a + 1].broadcast_to([P, GB]))
                        last.then_inc(init_ready, 1)

                def split(b):
                    pool.wait_ge(rcp_ready, b + 1)
                    if b >= 2:
                        pool.wait_ge(rt_done, b - 1)
                    s = r_s[:, b % 2]
                    chained(nc.gpsimd.tensor_scalar(r_f[:], rcp[:, b % 2, :], E2, None, ALU.mult))
                    chained(nc.gpsimd.tensor_copy(s[:, 0, :], r_f[:]))
                    chained(nc.gpsimd.tensor_tensor(r_d[:, 0, :], r_f[:], s[:, 0, :], ALU.subtract))
                    chained(nc.gpsimd.tensor_copy(s[:, 1, :], r_d[:, 0, :]))
                    nc.gpsimd.tensor_tensor(s[:, 2, :], r_d[:, 0, :], s[:, 1, :], ALU.subtract).then_inc(rs_ready, 1)

                def norms(b):
                    pool.wait_ge(mv2_ready, b + 1)
                    v = mv2[:, b, :, 1]
                    r = rstd2[:, b, :]
                    chained(nc.gpsimd.tensor_scalar(sq[:, 0, :], v, EPS, None, ALU.add))
                    nc.gpsimd.tensor_tensor(r, sq[:, 0, :], neg_half[:], ALU.pow).then_inc(rstd2_ready, 1)
                    pool.wait_ge(rstd2_ready, b + 1)
                    chained(nc.gpsimd.tensor_tensor(sq[:, 1, :], r, r, ALU.mult))
                    chained(nc.gpsimd.tensor_tensor(sq[:, 2, :], sq[:, 1, :], v, ALU.mult))
                    chained(nc.gpsimd.tensor_scalar(sq[:, 3, :], sq[:, 2, :], EPS, None, ALU.add))
                    nc.gpsimd.tensor_tensor(rstd3[:, b, :], sq[:, 3, :], neg_half[:], ALU.pow).then_inc(rstd3_ready, 1)

                for b in range(NB):
                    split(b)
                    norms(b)

            @block.scalar
            def _(act):
                act.dma_start(conv_w[:], conv[0:1, :].broadcast_to([P, 2 * CH])).then_inc(ld_emb, 16)
                act.dma_start(idn_b[:], ident_b).then_inc(ld_const, 16)
                act.dma_start(sel_b[:], sel).then_inc(ld_const, 16)

                def copy_out_prep(t):
                    act.wait_ge(prep_done, t + 1)
                    src = bank[4 + t % 2]
                    if t < N_POW:
                        dst = prep[t][0]
                        nc.scalar.activation(dst, src[:, 0:dst.shape[1]], ACT.Copy).then_inc(prep_ready, 1)
                    elif t < N_POW + NE:
                        nc.scalar.activation(out_w[:, t - N_POW, :, :].rearrange("p c o -> p (c o)"), src[:],
                                             ACT.Copy).then_inc(prep_ready, 1)
                    else:
                        nc.scalar.activation(attn_c[:], src[:, 0:1], ACT.Identity, bias=pa[:, PA["attn_b"]])
                        nc.scalar.activation(out_c[:], src[:, 1:1 + NE], ACT.Identity,
                                             bias=pa[:, PA["next_b"]]).then_inc(prep_ready, 1)

                def copy_step(g, i):
                    act.wait_ge(step_done[g], i + 1)
                    src = bank[(6, 0)[g] + i % 2][:, 0:NP * GB * NCH].rearrange("p (a k) -> p a k", k=NCH)
                    nc.scalar.activation(x_step(g, i), src, ACT.Copy).then_inc(x_ready[g], 1)
                    if i == T - 1:
                        nc.scalar.activation(E[:, g, :, 1:NCH],
                                             src[:, :, 0:NCH - 1],
                                             ACT.Copy).then_inc(ends_ready[g], 1)

                copied = 0
                act.wait_ge(ld_pa, 32)
                for b in range(NB + 1):
                    if b < NB:
                        act.wait_ge(gat_done, b + 1)
                        if b == 0:
                            act.wait_ge(tab_ready, 1)
                        nc.scalar.activation(h[:, b, :], bank[2][:], ACT.Relu, scale=scale_h[:]).then_inc(h_ready, 1)
                    for t in range(2 * b, min(2 * b + 2, N_POW)):
                        copy_out_prep(t)
                        copied = t + 1
                    if b >= 1:
                        act.wait_ge(u_t_done, b)
                        nc.scalar.activation(uT[:, b - 1, :, :].rearrange("p i k -> p (i k)"), bank[3][:],
                                             ACT.Copy).then_inc(uT_ready, 1)
                    if b >= GB + 1:
                        for i in range(3 * (b - GB - 1), 3 * (b - GB)):
                            copy_step(0, i)
                for r in range(T):
                    copy_step(1, r)
                    if G0_FRONT + r < T:
                        copy_step(0, G0_FRONT + r)
                    for t in range(copied + 2 * r, min(copied + 2 * r + 2, N_PREP)):
                        copy_out_prep(t)

                for j in range(-2, NB):
                    for n in range(8):
                        if j >= 0:
                            half, c = divmod(n, HC)
                            act.wait_ge(fc1_done, 8 * j + n + 1)
                            if j >= 1:
                                act.wait_ge(o_done, 2 * (j - 1) + half + 1)
                            e = expert(j, half)
                            nc.scalar.activation(hid[:, half, c, :], bank[5 + n % 2][:, 0:HALF], ACT.Gelu,
                                                 bias=pa[:, PA["fc1_b"]][:, e * HC + c:e * HC + c + 1]
                                                 ).then_inc(hid_ready, 1)
                        if n == 3 and j + 2 < NB:
                            b = j + 2
                            act.wait_ge(rt_done, b + 1)
                            if b >= 2:
                                act.wait_ge(R_done, 2 * (b - 1))
                            nc.scalar.activation(r_T[:, b % 2, :], bank_rt, ACT.Copy).then_inc(rT_ready, 1)
                        if n == 3 and 0 <= j + 1 < NB:
                            b = j + 1
                            act.wait_ge(xp_t_done, b + 1)
                            if b >= 2:
                                act.wait_ge(attn_done, b - 1)
                            nc.scalar.activation(xpT[:, b % 2, :], bank[3][:], ACT.Copy).then_inc(xpT_ready, 1)
                        if n == 6 and 0 <= j + 1 < NB:
                            b = j + 1
                            act.wait_ge(xa_t_done, b + 1)
                            if b >= 2:
                                act.wait_ge(fc1_done, 8 * (b - 1))
                            nc.scalar.activation(
                                xaT[:, b % 2, :, :].rearrange("p s (i k) -> p s i k", i=T),
                                bank[3][:].rearrange("p (i s k) -> p s i k", i=T, s=2),
                                ACT.Identity, bias=attn_c[:]).then_inc(xaT_ready, 1)
                    if j >= 0:
                        act.wait_ge(o_done, 2 * j + 2)
                        if j >= 2:
                            act.wait_ge(res_ready, j - 1)
                        for half in range(2):
                            e = expert(j, half)
                            s = slice(half * HALF, (half + 1) * HALF)
                            last = nc.scalar.activation(gel[:, j % 2, s], bank[7][:, s], ACT.Gelu,
                                                        bias=out_c[:, e:e + 1])
                        last.then_inc(gel_ready, 1)

            @block.vector
            def _(dve):
                link = [0]

                def chained(ins):
                    link[0] += 1
                    ins.then_inc(dve_link, 1)
                    dve.wait_ge(dve_link, link[0])

                dve.wait_ge(ld_ids, 16)
                nc.vector.tensor_scalar(ids_b[:], ids_i[:], -1.0, float(VOC - 1), ALU.max, ALU.min).then_inc(ids_ready, 1)
                dve.wait_ge(ld_emb, 32)
                nc.vector.tensor_reduce(amax_e[:], emb_w[:], AX.X, ALU.max,
                                        apply_absolute_value=True).then_inc(amax_e_ready, 1)
                chained(nc.vector.tensor_reduce(scale_c[:], conv_w[:], AX.X, ALU.max, apply_absolute_value=True))
                chained(nc.vector.tensor_scalar(scale_c[:], scale_c[:], 1.0 / QMAX, None, ALU.mult))
                chained(nc.vector.reciprocal(inv_c[:], scale_c[:]))
                chained(nc.vector.tensor_scalar(q_c[:], conv_w[:], inv_c[:], None, ALU.mult))
                chained(nc.vector.tensor_scalar(q_c[:], q_c[:], ROUND, -ROUND, ALU.add, ALU.add))
                dve.wait_ge(amax_t_done, 1)
                nc.vector.tensor_reduce(amax_row[:], bank[6][0:1, 0:VOC], AX.X, ALU.max).then_inc(amax_row_ready, 1)
                dve.wait_ge(amax_bc_done, 1)
                chained(nc.vector.tensor_scalar(scale_e[:], bank[7][:, 0:1], 1.0 / QMAX, None, ALU.mult))
                chained(nc.vector.reciprocal(inv_e[:], scale_e[:]))
                chained(nc.vector.tensor_scalar(q_e[:], emb_w[:], inv_e[0:VOC, :], None, ALU.mult))
                chained(nc.vector.tensor_scalar(q_e[:], q_e[:], ROUND, -ROUND, ALU.add, ALU.add))
                for tap in range(2):
                    last = nc.vector.tensor_tensor(prod[:, tap, :], q_e[:], q_c[0:VOC, tap * CH:(tap + 1) * CH], ALU.mult)
                chained(last)
                chained(nc.vector.tensor_copy(tab[:, 0], prod[:]))
                nc.vector.tensor_tensor(scale_h[:], scale_e[:], scale_c[:], ALU.mult)
                nc.vector.tensor_tensor(tab[:, 1], prod[:], tab[:, 0], ALU.subtract).then_inc(tab_ready, 1)

                def one_hot(b):
                    for s in range(2):
                        n = 2 * b + s
                        dve.wait_ge(idb_done, n + 1)
                        if b >= 2:
                            dve.wait_ge(gat_done, b - 1)
                        w = EXT * NCH // 2
                        nc.vector.tensor_scalar(onehot[:, b % 2, s * w:(s + 1) * w], bank[n % 2][0:VOC, 0:w],
                                                pa[0:VOC, PA["iota"]], None, ALU.is_equal).then_inc(oh_ready, 1)

                def normalise(dst, src, b, mv, rstd):
                    for q in range(NQ):
                        s = slice(q * CH, (q + 1) * CH)
                        last = nc.vector.tensor_scalar(dst[:, b % 2, s], src[:, b, s], mv[:, b, q, 0:1],
                                                       rstd[:, b, q:q + 1], ALU.subtract, ALU.mult)
                    return last

                def statistics(b, st, st_ready, mv, mv_ready):
                    for q in range(NQ):
                        last = nc.vector.bn_stats(st[:, b % 2, q, :], h[:, b, q * CH:(q + 1) * CH])
                    last.then_inc(st_ready, 1)
                    dve.wait_ge(st_ready, b + 1)
                    for q in range(NQ):
                        last = nc.vector.bn_aggr(mv[:, b, q, :], st[:, b % 2, q, :])
                    last.then_inc(mv_ready, 1)

                dve.wait_ge(ld_pa, 32)
                one_hot(0)
                for b in range(NB + 1):
                    if b + 1 < NB:
                        one_hot(b + 1)
                    if b >= 1:
                        dve.wait_ge(rstd1_ready, b)
                        if b >= 3:
                            dve.wait_ge(u_t_done, b - 2)
                        normalise(u, h, b - 1, mv1, rstd1).then_inc(u_ready, 1)
                    if b < NB:
                        dve.wait_ge(h_ready, b + 1)
                        statistics(b, st1, st1_ready, mv1, mv1_ready)
                dve.wait_ge(ld_pb, 16)
                nc.vector.tensor_scalar(attn_g[:], pb[:, PB["attn"]], pa[:, PA["ln_g"]], None,
                                        ALU.mult).then_inc(attn_g_ready, 1)

                def ks_add(g, lv):
                    dve.wait_ge(ks_done[g], lv + 1)
                    nc.vector.tensor_tensor(ks_dst(g, lv), ks_dst(g, lv), ks_bank(g, lv), ALU.add).then_inc(ks_ready[g], 1)

                def p2_add(g, i):
                    dve.wait_ge(p2_done[g], i + 1)
                    src = bank[(4, 6)[g] + i % 2][:, 0:NP * GB * NCH].rearrange("p (a k) -> p a k", k=NCH)
                    nc.vector.tensor_tensor(x_step(g, i), x_step(g, i), src, ALU.add).then_inc(x2_ready[g], 1)

                for lv in range(LEVELS):
                    ks_add(0, lv)
                for i in range(T):
                    p2_add(0, i)
                    if i >= T - 2 - LEVELS and i < T - 2:
                        ks_add(1, i - (T - 2 - LEVELS))

                for j in range(-2, NB + 1):
                    for n in range(8):
                        if j < 0:
                            p2_add(1, 8 * (j + 2) + n)
                        b = j + 2
                        if n == 0 and b < NB:
                            for a in range(NP):
                                dve.wait_ge(xt_done, 2 * b + a + 1)
                                last = nc.vector.tensor_reduce(
                                    amax[:, b % 2, :, 2 * a:2 * a + 2],
                                    bank[a][:].rearrange("p (q n d) -> p q n d", q=NQ, n=2), AX.X, ALU.max,
                                    apply_absolute_value=True)
                            last.then_inc(amax_ready, 1)
                            dve.wait_ge(amax_ready, b + 1)
                            if b >= 2:
                                dve.wait_ge(rs_ready, b - 1)
                            nc.vector.reciprocal(rcp[:, b % 2, :],
                                                 amax[:, b % 2, :, :].rearrange("p q n -> p (q n)")).then_inc(rcp_ready, 1)
                        if n == 1 and j >= 1:
                            o = j - 1
                            dve.wait_ge(gel_ready, o + 1)
                            dve.wait_ge(h2_t_done, o + 1)
                            if o >= 2:
                                dve.wait_ge(stored[o % 2], 16 * (o // 2))
                            view = "p (s i k) -> p s i k"
                            nc.vector.tensor_tensor(res[:, o % 2, :].rearrange(view, s=2, i=T),
                                                    gel[:, o % 2, :].rearrange(view, s=2, i=T),
                                                    bank[4][:].rearrange("p (i s k) -> p s i k", s=2, i=T),
                                                    ALU.add).then_inc(res_ready, 1)
                        b = j + 1
                        if n == 2 and 0 <= b < NB:
                            dve.wait_ge(rstd2_ready, b + 1)
                            if b >= 2:
                                dve.wait_ge(xp_t_done, b - 1)
                            normalise(xp, h, b, mv2, rstd2).then_inc(xp_ready, 1)
                        b = j + 2
                        if n == 5 and b < NB:
                            g, bb = divmod(b, GB)
                            for a in range(NP):
                                dve.wait_ge(R_done, 2 * b + a + 1)
                                if b >= 2:
                                    dve.wait_ge(y_done, b - 1)
                                nc.vector.tensor_tensor(xh[:, b % 2, a, :],
                                                        X[:, g, a * GB + bb, :, :].rearrange("p i k -> p (i k)"),
                                                        bank[a][:],
                                                        ALU.mult).then_inc(xh_ready, 1)
                        b = j + 1
                        if n == 5 and 0 <= b < NB:
                            dve.wait_ge(attn_done, b + 1)
                            dve.wait_ge(rstd3_ready, b + 1)
                            dve.wait_ge(xp_ready, b + 1)
                            if b >= 2:
                                dve.wait_ge(xa_t_done, b - 1)
                            for q in range(NQ):
                                s = slice(q * CH, (q + 1) * CH)
                                last = nc.vector.scalar_tensor_tensor(
                                    out=xa[:, b % 2, s], in0=bank[2][:, s], scalar=rstd3[:, b, q:q + 1],
                                    in1=xp[:, b % 2, s], op0=ALU.mult, op1=ALU.add)
                            last.then_inc(xa_ready, 1)
                        b = j + 2
                        if n == 7 and b < NB:
                            dve.wait_ge(y_done, b + 1)
                            nc.vector.tensor_tensor(h[:, b, :], h[:, b, :], bank[2][:], ALU.add).then_inc(h2_ready, 1)
                            dve.wait_ge(h2_ready, b + 1)
                            statistics(b, st2, st2_ready, mv2, mv2_ready)

            @block.tensor
            def _(pe):
                mm = nc.tensor.matmul

                def prepare(t):
                    if t >= 2:
                        pe.wait_ge(prep_ready, t - 1)
                    dst = bank[4 + t % 2]
                    if t < N_POW:
                        out_, lhs, rhs, need = prep[t]
                        if need > max(t - 1, 0):
                            pe.wait_ge(prep_ready, need)
                        last = mm(dst[:, 0:out_.shape[1]], lhs, rhs, start=True, stop=True)
                    elif t < N_POW + NE:
                        e = t - N_POW
                        pe.wait_ge(ld_pb, 16)
                        pe.wait_ge(ld_fc2, 16)
                        for c in range(HC):
                            last = mm(dst[:, c * CH:(c + 1) * CH], fc2_w[:, e * HID + c * P:e * HID + (c + 1) * P],
                                      pb[:, PB["nw"]], start=True, stop=True)
                    else:
                        mm(dst[:, 0:1], pb[:, PB["attn"]], pa[:, PA["ln_b"]], start=True, stop=True)
                        last = mm(dst[:, 1:1 + NE], pb[:, PB["nw"]], pa[:, PA["fc2_b"]], start=True, stop=True)
                    last.then_inc(prep_done, 1)

                def spread_ids(b):
                    for s in range(2):
                        n = 2 * b + s
                        if n >= 2:
                            pe.wait_ge(oh_ready, n - 1)
                        mm(bank[n % 2][:, 0:EXT * NCH // 2], rowsel[:, n, :], ids_b[:], start=True,
                           stop=True).then_inc(idb_done, 1)

                def gather(b):
                    pe.wait_ge(oh_ready, 2 * b + 2)
                    if b >= 1:
                        pe.wait_ge(h_ready, b)
                    for q in range(NQ):
                        for n, (tap, part) in enumerate([(0, 0), (0, 1), (1, 0), (1, 1)]):
                            at = (q * TQ + tap) * NCH
                            last = mm(bank[2][:, q * CH:(q + 1) * CH], onehot[:, b % 2, at:at + P], tab[:, part, tap, :],
                                      start=(n == 0), stop=(n == 3))
                    last.then_inc(gat_done, 1)

                def transpose_u(b):
                    pe.wait_ge(u_ready, b + 1)
                    if b >= 1:
                        pe.wait_ge(uT_ready, b)
                    for q in range(NQ):
                        s = slice(q * CH, (q + 1) * CH)
                        last = nc.tensor.transpose(bank[3][:, s], u[:, b % 2, s], ident)
                    last.then_inc(u_t_done, 1)

                def scan_step(g, i):
                    dst = bank[(6, 0)[g] + i % 2]
                    if i == 0:
                        pe.wait_ge(uT_ready, GB * (g + 1))
                    if i >= 2:
                        pe.wait_ge(x_ready[g], i - 1)
                    w = GB * NCH
                    for a in range(NP):
                        last = mm(dst[:, a * w:(a + 1) * w], pa[:, PA["b"]][:, a * P:(a + 1) * P], uT[:, g * GB:(g + 1) * GB, i, :],
                                  start=(a == 0), stop=(i == 0 and a == NP - 1))
                    if i >= 1:
                        pe.wait_ge(x_ready[g], i)
                        last = mm(dst[:, 0:NP * w], a1, x_step(g, i - 1), start=False, stop=True)
                    last.then_inc(step_done[g], 1)

                def ks_step(g, lv):
                    if lv == 0:
                        pe.wait_ge(init_ready, NG * NP)
                        pe.wait_ge(ends_ready[g], 1)
                        pe.wait_ge(prep_ready, N_POW)
                        pe.wait_ge(h_ready, NB)
                        pe.wait_ge(uT_ready, NB)
                    else:
                        pe.wait_ge(ks_ready[g], lv)
                    mm(ks_bank(g, lv), step_of(lv), ks_src(g, lv), start=True, stop=True).then_inc(ks_done[g], 1)

                def second_pass(g, i):
                    if i == 0:
                        pe.wait_ge(ks_ready[g], LEVELS)
                        pe.wait_ge(prep_ready, N_PREP)
                        pe.wait_ge(x_ready[0], T)
                    if i >= 2:
                        pe.wait_ge(x2_ready[g], i - 1)
                    mm(bank[(4, 6)[g] + i % 2][:, 0:NP * GB * NCH], a1 if i == 0 else pw[:, i + 1, :],
                       E[:, g, :, :].rearrange("p a k -> p (a k)"), start=True, stop=True).then_inc(p2_done[g], 1)

                pe.wait_ge(ld_pa, 32)
                pe.wait_ge(amax_e_ready, 1)
                nc.tensor.transpose(bank[6][0:1, 0:VOC], amax_e[:], ident[0:VOC, 0:VOC]).then_inc(amax_t_done, 1)
                pe.wait_ge(pool_const, 3)
                pe.wait_ge(ids_ready, 1)
                spread_ids(0)
                pe.wait_ge(amax_row_ready, 1)
                mm(bank[7][:, 0:1], ones1[:], amax_row[:], start=True, stop=True).then_inc(amax_bc_done, 1)
                prepared = 0
                for b in range(NB + 1):
                    if b + 1 < NB:
                        spread_ids(b + 1)
                    if b == 0:
                        pe.wait_ge(tab_ready, 1)
                    if b < NB:
                        gather(b)
                    for t in range(2 * b, min(2 * b + 2, N_POW)):
                        prepare(t)
                        prepared = t + 1
                    if b >= 1:
                        transpose_u(b - 1)
                    if b >= GB + 1:
                        for i in range(3 * (b - GB - 1), 3 * (b - GB)):
                            scan_step(0, i)
                p2 = 0
                for r in range(T):
                    scan_step(1, r)
                    if G0_FRONT + r < T:
                        scan_step(0, G0_FRONT + r)
                    for t in range(prepared + 2 * r, min(prepared + 2 * r + 2, N_PREP)):
                        prepare(t)
                    if KS0_AT <= r < P2_AT:
                        ks_step(0, r - KS0_AT)
                    if r >= P2_AT:
                        for i in range(p2, p2 + 1):
                            second_pass(0, i)
                        p2 += 1
                for i in range(p2, T):
                    second_pass(0, i)
                    if i >= T - 2 - LEVELS and i < T - 2:
                        ks_step(1, i - (T - 2 - LEVELS))

                def transpose_x(b):
                    g, bb = divmod(b, GB)
                    pe.wait_ge(x2_ready[g], T)
                    if b == 0:
                        pe.wait_ge(x_ready[1], T)
                    for a in range(NP):
                        if b >= 1:
                            pe.wait_ge(xh_ready, 2 * (b - 1) + a + 1)
                        for q in range(NQ):
                            last = nc.tensor.transpose(bank[a][:, q * P:(q + 1) * P],
                                                       X[:, g, a * GB + bb, q * TQ:(q + 1) * TQ, :].rearrange("p i k -> p (i k)"),
                                                       ident)
                        last.then_inc(xt_done, 1)

                def transpose_r(b):
                    pe.wait_ge(ld_const, 32)
                    pe.wait_ge(rs_ready, b + 1)
                    if b == 0:
                        pe.wait_ge(x2_ready[0], T)
                    if b >= 3:
                        pe.wait_ge(res_ready, b - 2)
                    nc.tensor.transpose(bank_rt, r_s[:, b % 2, :, :].rearrange("p s n -> p (s n)"),
                                        idn_b[:]).then_inc(rt_done, 1)

                def spread_r(b):
                    pe.wait_ge(rT_ready, b + 1)
                    pe.wait_ge(amax_ready, b + 1)
                    for a in range(NP):
                        for q in range(NQ):
                            n = q * NP + a
                            last = mm(bank[a][:, q * P:(q + 1) * P], sel_b[:, n * P:(n + 1) * P], r_T[:, b % 2, :],
                                      start=True, stop=True)
                        last.then_inc(R_done, 1)

                def mixer_out(b, q):
                    if q == 0:
                        pe.wait_ge(xh_ready, 2 * b + 2)
                        pe.wait_ge(ks_ready[0], LEVELS)
                        if b >= 1:
                            pe.wait_ge(xa_ready, b)
                    dst = bank[2][:, q * CH:(q + 1) * CH]
                    mm(dst, uT[:, b, q * TQ:(q + 1) * TQ, :].rearrange("p i k -> p (i k)"), pb[:, PB["d"]],
                       start=True, stop=False)
                    for a in range(NP):
                        last = mm(dst, xh[:, b % 2, a, q * P:(q + 1) * P], pb[:, PB["c"]][:, a * CH:(a + 1) * CH],
                                  start=False, stop=(a == NP - 1))
                    if q == NQ - 1:
                        last.then_inc(y_done, 1)

                def transpose_xp(b):
                    pe.wait_ge(xp_ready, b + 1)
                    if b == 0:
                        pe.wait_ge(ks_ready[1], LEVELS)
                    else:
                        pe.wait_ge(xaT_ready, b)
                    for q in range(NQ):
                        s = slice(q * CH, (q + 1) * CH)
                        last = nc.tensor.transpose(bank[3][:, s], xp[:, b % 2, s], ident)
                    last.then_inc(xp_t_done, 1)

                def attn(b):
                    pe.wait_ge(attn_g_ready, 1)
                    pe.wait_ge(xpT_ready, b + 1)
                    pe.wait_ge(h2_ready, b + 1)
                    for q in range(NQ):
                        s = slice(q * CH, (q + 1) * CH)
                        last = mm(bank[2][:, s], xpT[:, b % 2, s], attn_g[:], start=True, stop=True)
                    last.then_inc(attn_done, 1)

                def transpose_xa(b):
                    pe.wait_ge(xa_ready, b + 1)
                    for q in range(NQ):
                        s = slice(q * CH, (q + 1) * CH)
                        last = nc.tensor.transpose(bank[3][:, s], xa[:, b % 2, s], ident)
                    last.then_inc(xa_t_done, 1)

                def fc1_part(b, n):
                    half, c = divmod(n, HC)
                    e = expert(b, half)
                    if n == 0:
                        pe.wait_ge(xaT_ready, b + 1)
                        if b == 0:
                            pe.wait_ge(ld_fc1, 16)
                            pe.wait_ge(x2_ready[1], T)
                    if 8 * b + n >= 2:
                        pe.wait_ge(hid_ready, 8 * b + n - 1)
                    mm(bank[5 + n % 2][:, 0:HALF], fc1_w[:, e * HID + c * P:e * HID + (c + 1) * P],
                       xaT[:, b % 2, half, :], start=True, stop=True).then_inc(fc1_done, 1)

                def out_part(b, n):
                    half, c = divmod(n, HC)
                    e = expert(b, half)
                    if n == 0 and b >= 1:
                        pe.wait_ge(gel_ready, b)
                    pe.wait_ge(hid_ready, 8 * b + n + 1)
                    last = mm(bank[7][:, half * HALF:(half + 1) * HALF], out_w[:, e, c, :], hid[:, half, c, :],
                              start=(c == 0), stop=(c == HC - 1))
                    if c == HC - 1:
                        last.then_inc(o_done, 1)

                def transpose_h(b):
                    pe.wait_ge(rT_ready, min(b + 3, NB))
                    if b >= 1:
                        pe.wait_ge(res_ready, b)
                    for q in range(NQ):
                        s = slice(q * CH, (q + 1) * CH)
                        last = nc.tensor.transpose(bank[4][:, s], h[:, b, s], ident)
                    last.then_inc(h2_t_done, 1)

                for j in range(-2, NB):
                    for n in range(8):
                        if j < 0:
                            second_pass(1, 8 * (j + 2) + n)
                        else:
                            fc1_part(j, n)
                            if n >= 2:
                                out_part(j, n - 2)
                        if n == 0 and j + 2 < NB:
                            transpose_x(j + 2)
                        if n == 3 and j + 2 < NB:
                            transpose_r(j + 2)
                        if n == 3 and 0 <= j + 1 < NB:
                            transpose_xp(j + 1)
                        if n == 4 and j + 2 < NB:
                            spread_r(j + 2)
                        if n == 4 and 0 <= j + 1 < NB:
                            attn(j + 1)
                        if n == 6 and 0 <= j + 1 < NB:
                            transpose_xa(j + 1)
                        if n >= 6 and j + 2 < NB:
                            mixer_out(j + 2, 2 * (n - 6))
                            mixer_out(j + 2, 2 * (n - 6) + 1)
                    if j >= 0:
                        out_part(j, 6)
                        out_part(j, 7)
                        transpose_h(j)


def kernel(x, L0_tok_emb_weight, L0_tok_conv_weight, L0_attn_init_states, L0_attn_A, L0_attn_B, L0_attn_C,
           L0_attn_D, L0_ffn_ln_g, L0_ffn_ln_b, L0_ffn_attn_w, L0_ffn_attn_b, L0_ffn_gate_w, L0_ffn_fc1_w,
           L0_ffn_fc1_b, L0_ffn_fc2_w, L0_ffn_fc2_b, L0_ffn_next_w, L0_ffn_next_b):
    import concourse.bacc as bacc
    from concourse.bass_utils import run_bass_kernel_spmd
    import ml_dtypes

    f = lambda a: np.asarray(a)
    ids = f(x).reshape(NB, NCH, T).transpose(0, 2, 1)
    before = np.full((NB, 1, NCH), -1, ids.dtype)
    before[:, 0, 1:] = ids[:, T - 1, :-1]
    ids = np.concatenate([before, ids], 1).reshape(2 * NB, EXT * NCH // 2)

    def diag(a):
        out = np.zeros((P, P), a.dtype)
        out[:DH, :DH] = a
        out[DH:, DH:] = a
        return out

    A = f(L0_attn_A)
    parts = dict(
        a=diag(A), at=diag(A.T), ident=np.eye(P, dtype=np.float32), b=f(L0_attn_B),
        iota=np.arange(P, dtype=np.float32)[:, None],
        init=f(L0_attn_init_states).reshape(NP, P).T, ln_g=f(L0_ffn_ln_g)[:, None], ln_b=f(L0_ffn_ln_b)[:, None],
        attn_b=f(L0_ffn_attn_b)[:, None], next_b=f(L0_ffn_next_b)[:, None],
        fc1_b=f(L0_ffn_fc1_b).reshape(NE * HC, P).T, fc2_b=f(L0_ffn_fc2_b).T)
    pack_a = np.concatenate([parts[n] for n in PA_COLS], 1)
    parts = dict(nw=f(L0_ffn_next_w).T, c=f(L0_attn_C).reshape(NP, P, CH).transpose(1, 0, 2).reshape(P, NP * CH),
                 d=f(L0_attn_D), attn=f(L0_ffn_attn_w).T)
    pack_b = np.concatenate([parts[n] for n in PB_COLS], 1)
    sel = np.zeros((NS, NQ, NH, NQ, NP, 2, DH), ml_dtypes.bfloat16)
    for q in range(NQ):
        for n in range(NH):
            sel[:, q, n, q, n // 2, n % 2, :] = 1
    arrays = dict(
        ids=ids, emb=f(L0_tok_emb_weight), conv=f(L0_tok_conv_weight)[:, 0, :].T.reshape(1, 2 * CH),
        pack_a=pack_a, pack_b=pack_b, sel=sel.reshape(NS * NQ * NH, NQ * NP * P),
        ident_b=np.eye(P).astype(ml_dtypes.bfloat16),
        fc1=f(L0_ffn_fc1_w).transpose(2, 0, 1).reshape(P, NE * HID),
        fc2=f(L0_ffn_fc2_w).transpose(1, 0, 2))
    arrays = {n: np.ascontiguousarray(a) for n, a in arrays.items()}
    nc = bacc.Bacc("TRN2", target_bir_lowering=False, num_devices=1)
    args = {n: nc.dram_tensor(f"in_{n}", a.shape, mybir.dt.from_np(a.dtype), kind="ExternalInput").ap()
            for n, a in arrays.items()}
    out = nc.dram_tensor("out", (NB, P, L), F32, kind="ExternalOutput").ap()
    build(nc, out=out, **args)
    r = run_bass_kernel_spmd(nc, [{f"in_{n}": a for n, a in arrays.items()}], core_ids=[0])
    got = r.results[0]["out"].reshape(NB, CH, 2, T, NCH // 2)
    return np.ascontiguousarray(got.transpose(0, 2, 4, 3, 1)).reshape(NB, L, CH)
```

```python
from contextlib import ExitStack

import concourse.bass as bass
import numpy as np
from concourse import mybir

ALU = mybir.AluOpType
ACT = mybir.ActivationFunctionType
AX = mybir.AxisListType
F32 = mybir.dt.float32
BF16 = mybir.dt.bfloat16
F32R = mybir.dt.float32r
I32 = mybir.dt.int32

P = 128
NB = 8
L = 512
T = 16
NCH = L // T
NG = 2
GB = NB // NG
VOC = 125
NH, DH = 4, 64
NP = NH * DH // P
CH = 128
NE, HID = 8, 512
HC = HID // P
TQ = P // NCH
NQ = T // TQ
EXT = T + 1
HALF = L // 2
QMAX = 127.0
EPS = 1e-5
ROUND = 12582912.0
E2 = float(np.exp(np.float32(2.0)))
NS = 2
LEVELS = NCH.bit_length() - 1

PA_COLS = dict(a=P, at=P, b=NP * P, init=NP, ln_g=1, ln_b=1, attn_b=1, next_b=1,
               fc1_b=NE * HC, fc2_b=NE)
PC_COLS = dict(ident=P, iota=1)
PB_COLS = dict(nw=CH, c=NP * CH, d=CH, attn=CH)


def spans(cols):
    out, at = {}, 0
    for name, n in cols.items():
        out[name] = slice(at, at + n)
        at += n
    return out, at


PA, PA_N = spans(PA_COLS)
PB, PB_N = spans(PB_COLS)
PC, PC_N = spans(PC_COLS)


def build(nc, ids, rows, emb, conv, pack_a, pack_b, pack_c, sel, fc1, fc2, out):
    with ExitStack() as ctx:
        def sb(name, shape, dt=F32):
            return ctx.enter_context(nc.sbuf_tensor(name, shape, dt))

        def sem(name):
            return ctx.enter_context(nc.semaphore(name))

        ids_i = sb("ids_i", [2 * NB, EXT * NCH // 2], I32)
        ids_b = sb("ids_b", [2 * NB, EXT * NCH // 2], BF16)
        rowsel = sb("rowsel", [2 * NB, 2 * NB, P], BF16)
        emb_w = sb("emb_w", [VOC, CH])
        conv_w = sb("conv_w", [P, 2 * CH])
        pa = sb("pa", [P, PA_N])
        pc = sb("pc", [P, PC_N])
        pb = sb("pb", [P, PB_N])
        sel_f = sb("sel_f", [NS * NQ * NH, NQ * NP * P])
        sel_r = sb("sel_r", [NS * NQ * NH, NQ * NP * P], F32R)
        fc1_w = sb("fc1_w", [P, NE * HID])
        fc2_w = sb("fc2_w", [P, NE * HID])
        out_w = sb("out_w", [P, NE, HC, CH])
        ones1 = sb("ones1", [1, P])
        neg_half = sb("neg_half", [P, 2 * NQ])
        inv_e = sb("inv_e", [P, 1])
        inv_c = sb("inv_c", [P, 1])
        warm = sb("warm", [1, 1])
        amax_e = sb("amax_e", [VOC, 1])
        amax_row = sb("amax_row", [1, 1])
        scale_e = sb("scale_e", [P, 1])
        scale_c = sb("scale_c", [P, 1])
        scale_h = sb("scale_h", [P, 1])
        q_e = sb("q_e", [VOC, CH])
        q_c = sb("q_c", [P, 2 * CH])
        prod = sb("prod", [VOC, 2, CH])
        tab = sb("tab", [VOC, 2, 2, CH], BF16)
        onehot = sb("onehot", [VOC, 2, EXT * NCH], BF16)
        h = sb("h", [P, NB, NQ * CH])
        st1 = sb("st1", [P, 2, NQ, 6])
        mv1 = sb("mv1", [P, NB, NQ, 2])
        rstd1 = sb("rstd1", [P, NB, NQ])
        shift1 = sb("shift1", [P, NB, NQ])
        tmp1 = sb("tmp1", [P, 2, NQ])
        u = sb("u", [P, 2, NQ * CH])
        uT = sb("uT", [P, NB, T, NCH])
        pw = sb("pw", [P, T + 1, P])
        pw_t = sb("pw_t", [P, T.bit_length(), P])
        pk = sb("pk", [P, LEVELS, P])
        pk_t = sb("pk_t", [P, LEVELS, P])
        attn_g = sb("attn_g", [P, CH])
        attn_c = sb("attn_c", [P, 1])
        out_c = sb("out_c", [P, NE])
        X = sb("X", [P, NG, NP * GB, T, NCH])
        corr = sb("corr", [P, 2, NP * GB, NCH])
        E = sb("E", [P, NG, NP * GB, NCH])
        amax = sb("amax", [P, 2, NQ, NH])
        rcp = sb("rcp", [P, 2, NQ * NH])
        r_s = sb("r_s", [P, 2, NS, NQ * NH])
        r_T = sb("r_T", [NS * NQ * NH, 2, P], F32R)
        xh = sb("xh", [P, 2, NP, L])
        st2 = sb("st2", [P, 2, NQ, 6])
        mv2 = sb("mv2", [P, NB, NQ, 2])
        sq = sb("sq", [P, 2, 4, NQ])
        rstd2 = sb("rstd2", [P, NB, 2, NQ])
        xp = sb("xp", [P, 2, NQ * CH])
        xpT = sb("xpT", [P, 2, L])
        xa = sb("xa", [P, 2, NQ * CH])
        xaT = sb("xaT", [P, 2, 2, HALF])
        hid = sb("hid", [P, 2, HC, HALF])
        gel = sb("gel", [P, 2, L])
        res = sb("res", [P, 2, L])
        bank = [ctx.enter_context(nc.psum_tensor(f"bank{n}", [P, 512], F32)) for n in range(8)]
        bank_rt = bank[4][0:NS * NQ * NH, 0:P]

        ident = pc[:, PC["ident"]]

        ld_ids, ld_emb, ld_pa, ld_pb = sem("ld_ids"), sem("ld_emb"), sem("ld_pa"), sem("ld_pb")
        ld_pc, ld_sel, ld_fc1, ld_fc2 = sem("ld_pc"), sem("ld_sel"), sem("ld_fc1"), sem("ld_fc2")
        sel_ready, v2_ready, ld_conv = sem("sel_ready"), sem("v2_ready"), sem("ld_conv")
        pool_const = sem("pool_const")
        pool_link, dve_link = sem("pool_link"), sem("dve_link")
        ids_ready, amax_e_ready, amax_row_ready, tab_ready = (
            sem("ids_ready"), sem("amax_e_ready"), sem("amax_row_ready"), sem("tab_ready"))
        attn_g_ready, scale_c_ready, q_c_ready = sem("attn_g_ready"), sem("scale_c_ready"), sem("q_c_ready")
        amax_t_done, amax_bc_done = sem("amax_t_done"), sem("amax_bc_done")
        idb_done, oh_ready, gat_done, h_ready = sem("idb_done"), sem("oh_ready"), sem("gat_done"), sem("h_ready")
        st1_ready, mv1_ready, rstd1_ready, u_ready = (
            sem("st1_ready"), sem("mv1_ready"), sem("rstd1_ready"), sem("u_ready"))
        u_act_ready = sem("u_act_ready")
        u_t_done, uT_ready = sem("u_t_done"), sem("uT_ready")
        prep_done, prep_ready = sem("prep_done"), sem("prep_ready")
        step_done, x_ready = [sem(f"step_done{g}") for g in range(NG)], [sem(f"x_ready{g}") for g in range(NG)]
        fused_done, fused_ready, corr_ready = sem("fused_done"), sem("fused_ready"), sem("corr_ready")
        init_ready, ends_ready = sem("init_ready"), [sem(f"ends_ready{g}") for g in range(NG)]
        ks_done, ks_ready = [sem(f"ks_done{g}") for g in range(NG)], [sem(f"ks_ready{g}") for g in range(NG)]
        p2_done, x2_ready = [sem(f"p2_done{g}") for g in range(NG)], [sem(f"x2_ready{g}") for g in range(NG)]
        xt_done, amax_ready, rs_ready = sem("xt_done"), sem("amax_ready"), sem("rs_ready")
        rt_done, rT_ready, R_done, xh_ready = sem("rt_done"), sem("rT_ready"), sem("R_done"), sem("xh_ready")
        y_done, h2_ready, st2_ready, mv2_ready = sem("y_done"), sem("h2_ready"), sem("st2_ready"), sem("mv2_ready")
        rstd2_ready, xp_ready = sem("rstd2_ready"), sem("xp_ready")
        xp_t_done, xpT_ready, attn_done, xa_ready = (
            sem("xp_t_done"), sem("xpT_ready"), sem("attn_done"), sem("xa_ready"))
        xa_t_done, xaT_ready = sem("xa_t_done"), sem("xaT_ready")
        fc1_done, hid_ready, o_done, gel_ready = sem("fc1_done"), sem("hid_ready"), sem("o_done"), sem("gel_ready")
        h2_t_done, res_ready = sem("h2_t_done"), sem("res_ready")
        stored = [sem("stored0"), sem("stored1")]

        def powers(n0, n1):
            return pw[:, n0:n1 + 1, :].rearrange("p n m -> p (n m)")

        a1, a1t = pa[:, PA["a"]], pa[:, PA["at"]]
        prep = [
            (powers(2, 2), a1t, a1, 0), (pw_t[:, 1, :], a1, a1t, 0),
            (pw[:, 3, :], pw_t[:, 1, :], a1, 2), (pw[:, 4, :], pw_t[:, 1, :], pw[:, 2, :], 2),
            (pw_t[:, 2, :], pw[:, 2, :], pw_t[:, 1, :], 2),
            (powers(5, 8), pw_t[:, 2, :], powers(1, 4), 5), (pw_t[:, 3, :], pw[:, 4, :], pw_t[:, 2, :], 5),
            (powers(9, 12), pw_t[:, 3, :], powers(1, 4), 7), (powers(13, 16), pw_t[:, 3, :], powers(5, 8), 7),
            (pw_t[:, 4, :], pw[:, 8, :], pw_t[:, 3, :], 7),
        ]
        prev, prev_t = pw[:, T, :], pw_t[:, 4, :]
        for lv in range(1, LEVELS):
            need = len(prep)
            prep.append((pk[:, lv, :], prev_t, prev, need))
            if lv < LEVELS - 1:
                prep.append((pk_t[:, lv, :], prev, prev_t, need))
            prev, prev_t = pk[:, lv, :], pk_t[:, lv, :]
        N_POW = len(prep)
        N_PREP = N_POW + 1

        def step_of(n):
            return pw[:, T, :] if n == 0 else pk[:, n, :]

        def ks_src(g, lv):
            return E[:, g, :, 0:NCH - 2 ** lv]

        def ks_dst(g, lv):
            return E[:, g, :, 2 ** lv:NCH]

        def ks_bank(g, lv):
            n = NP * GB * (NCH - 2 ** lv)
            return bank[(2, 3)[g]][:, 0:n].rearrange("p (a k) -> p a k", a=NP * GB)

        def x_step(g, i):
            return X[:, g, :, i, :]

        def expert(b, half):
            return (2 * b + half) % NE

        G0_FIRST = 6
        G0_ROUND = 3
        G0_FRONT = G0_ROUND * (NB + 2 - G0_FIRST)

        def embed_round_steps(b):
            return range(G0_ROUND * (b - G0_FIRST), G0_ROUND * (b - G0_FIRST + 1)) if b >= G0_FIRST else ()

        WITH_SECOND = T // 2
        G1_LEFT = LEVELS + WITH_SECOND
        group1_work = ([("step", i) for i in range(G1_LEFT, T)] + [("doubling", lv) for lv in range(LEVELS)]
                       + [("second", i) for i in range(T)])

        def group1_at(j, n):
            return group1_work[8 * (j + 3) + n]

        P2_BANKS = ((4, 5, 0, 1), (6, 7))

        def fused_at(j, n):
            slots = ((-3, 2), (-3, 4), (-3, 6), (-2, 0), (-2, 3), (-2, 6), (-1, 0), (-1, 3))
            return slots.index((j, n)) if (j, n) in slots else None

        def max_slot(j):
            return 0 if j == -3 else 4

        def second_bank(g, i):
            return bank[P2_BANKS[g][i % len(P2_BANKS[g])]][:, 0:NP * GB * NCH]

        assert len(group1_work) == 24

        with nc.Block() as block:

            @block.sync
            def _(sp):
                sp.dma_start(emb_w[:], emb).then_inc(ld_emb, 16)
                sp.dma_start(ids_i[:], ids).then_inc(ld_ids, 16)
                sp.dma_start(rowsel[:].rearrange("r j p -> r (j p)"), rows).then_inc(ld_ids, 16)
                sp.dma_start(pa[:], pack_a).then_inc(ld_pa, 16)
                sp.dma_start(pw[:, 1, :], pack_a[:, PA["a"]]).then_inc(ld_pa, 16)
                sp.dma_start(pb[:], pack_b).then_inc(ld_pb, 16)
                sp.dma_start(fc2_w[:].rearrange("p (e m) -> p e m", e=NE), fc2).then_inc(ld_fc2, 16)
                sp.dma_start(sel_f[:], sel).then_inc(ld_sel, 16)
                sp.dma_start(fc1_w[:], fc1).then_inc(ld_fc1, 16)
                for b in range(NB):
                    sp.wait_ge(res_ready, b + 1)
                    sp.dma_start(out[b], res[:, b % 2, :]).then_inc(stored[b % 2], 16)
                for s in range(2):
                    sp.wait_ge(stored[s], 16 * (NB // 2))

            @block.gpsimd
            def _(pool):
                nc.gpsimd.memset(ones1[:], 1.0).then_inc(pool_const, 1)
                nc.gpsimd.memset(neg_half[:], -0.5).then_inc(pool_const, 1)
                link = [0]

                def chained(ins):
                    link[0] += 1
                    ins.then_inc(pool_link, 1)
                    pool.wait_ge(pool_link, link[0])

                pool.wait_ge(pool_const, 2)
                pool.wait_ge(ld_pa, 32)
                for g in range(NG):
                    for a in range(NP):
                        nc.gpsimd.tensor_copy(E[:, g, a * GB:(a + 1) * GB, 0],
                                              pa[:, PA["init"]][:, a:a + 1].broadcast_to([P, GB])).then_inc(init_ready, 1)
                for b in range(NB):
                    pool.wait_ge(mv1_ready, b + 1)
                    r = rstd1[:, b, :]
                    chained(nc.gpsimd.tensor_scalar(tmp1[:, 0, :], mv1[:, b, :, 1], EPS, None, ALU.add))
                    chained(nc.gpsimd.tensor_tensor(r, tmp1[:, 0, :], neg_half[:, 0:NQ], ALU.pow))
                    chained(nc.gpsimd.tensor_tensor(tmp1[:, 1, :], mv1[:, b, :, 0], r, ALU.mult))
                    nc.gpsimd.tensor_scalar(shift1[:, b, :], tmp1[:, 1, :], -1.0, None, ALU.mult).then_inc(rstd1_ready, 1)
                pool.wait_ge(ld_sel, 16)
                nc.gpsimd.tensor_copy(sel_r[:], sel_f[:]).then_inc(sel_ready, 1)
                for j in range(-3, NB - 2):
                    for n in range(8):
                        if j < 0:
                            what, i = group1_at(j, n)
                            if what == "second":
                                pool.wait_ge(corr_ready, i + 1)
                                nc.gpsimd.tensor_tensor(x_step(1, i), x_step(1, i), corr[:, i % 2],
                                                        ALU.add).then_inc(x2_ready[1], 1)
                        b = j + 2
                        if n == 5 and b >= 0:
                            pool.wait_ge(v2_ready, b + 1)
                            nc.gpsimd.tensor_tensor(rstd2[:, b, :, :].rearrange("p s q -> p (s q)"),
                                                    sq[:, b % 2, 2:4, :].rearrange("p s q -> p (s q)"), neg_half[:],
                                                    ALU.pow).then_inc(rstd2_ready, 1)

            @block.scalar
            def _(act):
                act.dma_start(conv_w[:], conv[0:1, :].broadcast_to([P, 2 * CH])).then_inc(ld_conv, 16)
                act.dma_start(pc[:], pack_c).then_inc(ld_pc, 16)
                act.wait_ge(pool_const, 1)
                nc.scalar.activation(warm[:], ones1[0:1, 0:1], ACT.Gelu)

                def copy_out_prep(t):
                    act.wait_ge(prep_done, t + 1)
                    src = bank[4 + t % 2]
                    if t < N_POW:
                        dst = prep[t][0]
                        nc.scalar.activation(dst, src[:, 0:dst.shape[1]], ACT.Copy).then_inc(prep_ready, 1)
                    else:
                        nc.scalar.activation(attn_c[:], src[:, 0:1], ACT.Identity, bias=pa[:, PA["attn_b"]])
                        nc.scalar.activation(out_c[:], src[:, 1:1 + NE], ACT.Identity,
                                             bias=pa[:, PA["next_b"]]).then_inc(prep_ready, 1)

                def copy_step(g, i):
                    act.wait_ge(step_done[g], i + 1)
                    src = bank[6 + i % 2][:, 0:NP * GB * NCH].rearrange("p (a k) -> p a k", k=NCH)
                    nc.scalar.activation(x_step(g, i), src, ACT.Copy).then_inc(x_ready[g], 1)
                    if i == T - 1:
                        nc.scalar.activation(E[:, g, :, 1:NCH],
                                             src[:, :, 0:NCH - 1],
                                             ACT.Copy).then_inc(ends_ready[g], 1)

                copied = 0
                act.wait_ge(ld_pa, 32)
                for b in range(NB + 2):
                    if b < NB:
                        act.wait_ge(gat_done, b + 1)
                        if b == 0:
                            act.wait_ge(tab_ready, 1)
                        nc.scalar.activation(h[:, b, :], bank[2][:], ACT.Relu, scale=scale_h[:]).then_inc(h_ready, 1)
                    if b >= 2:
                        act.wait_ge(u_t_done, b - 1)
                        nc.scalar.activation(uT[:, b - 2, :, :].rearrange("p i k -> p (i k)"), bank[3][:],
                                             ACT.Copy).then_inc(uT_ready, 1)
                    for t in range(2 * b, min(2 * b + 2, N_POW)):
                        copy_out_prep(t)
                        copied = t + 1
                    if 1 <= b <= NB:
                        act.wait_ge(rstd1_ready, b)
                        if b == 1:
                            act.wait_ge(h_ready, 1)
                        if b >= 3:
                            act.wait_ge(u_t_done, b - 2)
                        for q in range(NQ // 2, NQ):
                            s = slice(q * CH, (q + 1) * CH)
                            last = nc.scalar.activation(u[:, (b - 1) % 2, s], h[:, b - 1, s], ACT.Identity,
                                                        scale=rstd1[:, b - 1, q:q + 1], bias=shift1[:, b - 1, q:q + 1])
                        last.then_inc(u_act_ready, 1)
                    for i in embed_round_steps(b):
                        copy_step(0, i)
                for i in range(G0_FRONT, T):
                    copy_step(0, i)
                    for t in range(copied, min(copied + 2, N_PREP)):
                        copy_out_prep(t)
                        copied = t + 1
                for lv in range(LEVELS):
                    copy_step(1, lv)
                    if copied < N_PREP:
                        copy_out_prep(copied)
                        copied += 1
                for i in range(LEVELS, G1_LEFT):
                    copy_step(1, i)

                for j in range(-3, NB):
                    for n in range(8):
                        if j < 0:
                            what, i = group1_at(j, n)
                            if what == "step":
                                copy_step(1, i)
                            if what == "second":
                                act.wait_ge(p2_done[1], i + 1)
                                if i >= 2:
                                    act.wait_ge(x2_ready[1], i - 1)
                                nc.scalar.activation(corr[:, i % 2], second_bank(1, i).rearrange(
                                    "p (a k) -> p a k", k=NCH), ACT.Copy).then_inc(corr_ready, 1)
                            e = fused_at(j, n)
                            if e is not None:
                                act.wait_ge(fused_done, e + 1)
                                nc.scalar.activation(out_w[:, e, :, :].rearrange("p c o -> p (c o)"), bank[5][:],
                                                     ACT.Copy).then_inc(fused_ready, 1)
                        if j >= 0:
                            half, c = divmod(n, HC)
                            act.wait_ge(fc1_done, 8 * j + n + 1)
                            if j >= 1:
                                act.wait_ge(o_done, 2 * (j - 1) + half + 1)
                            e = expert(j, half)
                            nc.scalar.activation(hid[:, half, c, :], bank[5 + n % 2][:, 0:HALF], ACT.Gelu,
                                                 bias=pa[:, PA["fc1_b"]][:, e * HC + c:e * HC + c + 1]
                                                 ).then_inc(hid_ready, 1)
                        b = j + 1
                        if n == 0 and 0 <= b < NB:
                            act.wait_ge(xp_t_done, b + 1)
                            if b >= 2:
                                act.wait_ge(attn_done, b - 1)
                            nc.scalar.activation(xpT[:, b % 2, :], bank[3][:], ACT.Copy).then_inc(xpT_ready, 1)
                        if n == 7 and 0 <= b < NB:
                            act.wait_ge(xa_t_done, b + 1)
                            if b >= 2:
                                act.wait_ge(fc1_done, 8 * (b - 1))
                            nc.scalar.activation(
                                xaT[:, b % 2, :, :].rearrange("p s (i k) -> p s i k", i=T),
                                bank[3][:].rearrange("p (i s k) -> p s i k", i=T, s=2),
                                ACT.Identity, bias=attn_c[:]).then_inc(xaT_ready, 1)
                        b = j + 3
                        if n == 7 and b < NB:
                            act.wait_ge(rt_done, b + 1)
                            if b >= 2:
                                act.wait_ge(R_done, 2 * (b - 1))
                            nc.scalar.activation(r_T[:, b % 2, :], bank_rt, ACT.Copy).then_inc(rT_ready, 1)
                    if j >= 0:
                        act.wait_ge(o_done, 2 * j + 2)
                        if j >= 2:
                            act.wait_ge(res_ready, j - 1)
                        for half in range(2):
                            e = expert(j, half)
                            s = slice(half * HALF, (half + 1) * HALF)
                            last = nc.scalar.activation(gel[:, j % 2, s], bank[7][:, s], ACT.Gelu,
                                                        bias=out_c[:, e:e + 1])
                        last.then_inc(gel_ready, 1)

            @block.vector
            def _(dve):
                link = [0]

                def chained(ins):
                    link[0] += 1
                    ins.then_inc(dve_link, 1)
                    dve.wait_ge(dve_link, link[0])

                dve.wait_ge(ld_emb, 16)
                nc.vector.tensor_reduce(amax_e[:], emb_w[:], AX.X, ALU.max,
                                        apply_absolute_value=True).then_inc(amax_e_ready, 1)
                dve.wait_ge(ld_conv, 16)
                chained(nc.vector.tensor_reduce(scale_c[:], conv_w[:], AX.X, ALU.max, apply_absolute_value=True))
                nc.vector.tensor_scalar(scale_c[:], scale_c[:], 1.0 / QMAX, None, ALU.mult).then_inc(scale_c_ready, 1)
                dve.wait_ge(amax_t_done, 1)
                nc.vector.tensor_reduce(amax_row[:], bank[6][0:1, 0:VOC], AX.X, ALU.max).then_inc(amax_row_ready, 1)
                dve.wait_ge(scale_c_ready, 1)
                chained(nc.vector.reciprocal(inv_c[:], scale_c[:]))
                chained(nc.vector.tensor_scalar(q_c[:], conv_w[:], inv_c[:], None, ALU.mult))
                nc.vector.tensor_scalar(q_c[:], q_c[:], ROUND, -ROUND, ALU.add, ALU.add).then_inc(q_c_ready, 1)
                dve.wait_ge(ld_ids, 32)
                nc.vector.tensor_scalar(ids_b[:], ids_i[:], -1.0, float(VOC - 1), ALU.max, ALU.min).then_inc(ids_ready, 1)
                dve.wait_ge(amax_bc_done, 1)
                chained(nc.vector.tensor_scalar(scale_e[:], bank[7][:, 0:1], 1.0 / QMAX, None, ALU.mult))
                chained(nc.vector.reciprocal(inv_e[:], scale_e[:]))
                chained(nc.vector.tensor_scalar(q_e[:], emb_w[:], inv_e[0:VOC, :], None, ALU.mult))
                chained(nc.vector.tensor_scalar(q_e[:], q_e[:], ROUND, -ROUND, ALU.add, ALU.add))
                dve.wait_ge(q_c_ready, 1)
                for tap in range(2):
                    last = nc.vector.tensor_tensor(prod[:, tap, :], q_e[:], q_c[0:VOC, tap * CH:(tap + 1) * CH], ALU.mult)
                chained(last)
                chained(nc.vector.tensor_copy(tab[:, 0], prod[:]))
                nc.vector.tensor_tensor(scale_h[:], scale_e[:], scale_c[:], ALU.mult)
                nc.vector.tensor_tensor(tab[:, 1], prod[:], tab[:, 0], ALU.subtract).then_inc(tab_ready, 1)

                def one_hot(b):
                    for s in range(2):
                        n = 2 * b + s
                        dve.wait_ge(idb_done, n + 1)
                        if b >= 2:
                            dve.wait_ge(gat_done, b - 1)
                        w = EXT * NCH // 2
                        nc.vector.tensor_scalar(onehot[:, b % 2, s * w:(s + 1) * w], bank[n % 2][0:VOC, 0:w],
                                                pc[0:VOC, PC["iota"]], None, ALU.is_equal).then_inc(oh_ready, 1)

                def normalise(dst, src, b, mv, rstd):
                    for q in range(NQ):
                        s = slice(q * CH, (q + 1) * CH)
                        last = nc.vector.tensor_scalar(dst[:, b % 2, s], src[:, b, s], mv[:, b, q, 0:1],
                                                       rstd[:, b, 0, q:q + 1], ALU.subtract, ALU.mult)
                    return last

                def statistics(b, st, st_ready, mv, mv_ready):
                    for q in range(NQ):
                        last = nc.vector.bn_stats(st[:, b % 2, q, :], h[:, b, q * CH:(q + 1) * CH])
                    last.then_inc(st_ready, 1)
                    dve.wait_ge(st_ready, b + 1)
                    for q in range(NQ):
                        last = nc.vector.bn_aggr(mv[:, b, q, :], st[:, b % 2, q, :])
                    last.then_inc(mv_ready, 1)

                dve.wait_ge(ld_pc, 16)
                one_hot(0)
                for b in range(NB + 1):
                    if b + 1 < NB:
                        one_hot(b + 1)
                    if b < NB:
                        dve.wait_ge(h_ready, b + 1)
                        statistics(b, st1, st1_ready, mv1, mv1_ready)
                    if b >= 1:
                        dve.wait_ge(rstd1_ready, b)
                        if b >= 3:
                            dve.wait_ge(u_t_done, b - 2)
                        for q in range(NQ // 2):
                            s = slice(q * CH, (q + 1) * CH)
                            last = nc.vector.tensor_scalar(u[:, (b - 1) % 2, s], h[:, b - 1, s],
                                                           mv1[:, b - 1, q, 0:1], rstd1[:, b - 1, q:q + 1],
                                                           ALU.subtract, ALU.mult)
                        last.then_inc(u_ready, 1)
                dve.wait_ge(ld_pb, 16)
                dve.wait_ge(ld_pa, 32)
                nc.vector.tensor_scalar(attn_g[:], pb[:, PB["attn"]], pa[:, PA["ln_g"]], None,
                                        ALU.mult).then_inc(attn_g_ready, 1)

                def ks_add(g, lv):
                    dve.wait_ge(ks_done[g], lv + 1)
                    nc.vector.tensor_tensor(ks_dst(g, lv), ks_dst(g, lv), ks_bank(g, lv), ALU.add).then_inc(ks_ready[g], 1)

                def p2_add(i):
                    dve.wait_ge(p2_done[0], i + 1)
                    src = second_bank(0, i).rearrange("p (a k) -> p a k", k=NCH)
                    nc.vector.tensor_tensor(x_step(0, i), x_step(0, i), src, ALU.add).then_inc(x2_ready[0], 1)

                for lv in range(LEVELS):
                    ks_add(0, lv)
                for i in range(T):
                    p2_add(i)

                for j in range(-3, NB + 1):
                    for n in range(8):
                        if j < 0:
                            what, i = group1_at(j, n)
                            if what == "doubling":
                                ks_add(1, i)
                        b = j + 2
                        if n == 0 and 0 <= b < NB:
                            g, bb = divmod(b, GB)
                            for a in range(NP):
                                dve.wait_ge(R_done, 2 * b + a + 1)
                                if b >= 2:
                                    dve.wait_ge(y_done, b - 1)
                                nc.vector.tensor_tensor(xh[:, b % 2, a, :],
                                                        X[:, g, a * GB + bb, :, :].rearrange("p i k -> p (i k)"),
                                                        bank[a][:], ALU.mult).then_inc(xh_ready, 1)
                        if n == 1 and j >= 1:
                            o = j - 1
                            dve.wait_ge(gel_ready, o + 1)
                            dve.wait_ge(h2_t_done, o + 1)
                            if o >= 2:
                                dve.wait_ge(stored[o % 2], 16 * (o // 2))
                            view = "p (s i k) -> p s i k"
                            nc.vector.tensor_tensor(res[:, o % 2, :].rearrange(view, s=2, i=T),
                                                    gel[:, o % 2, :].rearrange(view, s=2, i=T),
                                                    bank[4][:].rearrange("p (i s k) -> p s i k", s=2, i=T),
                                                    ALU.add).then_inc(res_ready, 1)
                        if n == 2 and 0 <= b < NB:
                            dve.wait_ge(y_done, b + 1)
                            nc.vector.tensor_tensor(h[:, b, :], h[:, b, :], bank[2][:], ALU.add).then_inc(h2_ready, 1)
                            dve.wait_ge(h2_ready, b + 1)
                            statistics(b, st2, st2_ready, mv2, mv2_ready)
                            if b >= 2:
                                dve.wait_ge(rstd2_ready, b - 1)
                            dve.wait_ge(mv2_ready, b + 1)
                            v, t = mv2[:, b, :, 1], sq[:, b % 2]
                            chained(nc.vector.tensor_scalar(t[:, 2, :], v, EPS, None, ALU.add))
                            chained(nc.vector.reciprocal(t[:, 0, :], t[:, 2, :]))
                            chained(nc.vector.tensor_tensor(t[:, 1, :], t[:, 0, :], v, ALU.mult))
                            nc.vector.tensor_scalar(t[:, 3, :], t[:, 1, :], EPS, None, ALU.add).then_inc(v2_ready, 1)
                        b = j + 3
                        if n == max_slot(j) and b < NB:
                            for a in range(NP):
                                dve.wait_ge(xt_done, 2 * b + a + 1)
                                last = nc.vector.tensor_reduce(
                                    amax[:, b % 2, :, 2 * a:2 * a + 2],
                                    bank[a][:].rearrange("p (q n d) -> p q n d", q=NQ, n=2), AX.X, ALU.max,
                                    apply_absolute_value=True)
                            last.then_inc(amax_ready, 1)
                            dve.wait_ge(amax_ready, b + 1)
                            chained(nc.vector.reciprocal(rcp[:, b % 2, :],
                                                         amax[:, b % 2, :, :].rearrange("p q n -> p (q n)")))
                            if b >= 2:
                                dve.wait_ge(rt_done, b - 1)
                            hi = r_s[:, b % 2, 0, :]
                            chained(nc.vector.tensor_scalar(hi.bitcast(F32R), rcp[:, b % 2, :], E2, None, ALU.mult))
                            nc.vector.scalar_tensor_tensor(out=r_s[:, b % 2, 1, :], in0=rcp[:, b % 2, :], scalar=E2,
                                                           in1=hi, op0=ALU.mult, op1=ALU.subtract).then_inc(rs_ready, 1)
                        b = j + 1
                        if n == 5 and 0 <= b < NB:
                            dve.wait_ge(attn_done, b + 1)
                            dve.wait_ge(xp_ready, b + 1)
                            if b >= 2:
                                dve.wait_ge(xa_t_done, b - 1)
                            for q in range(NQ):
                                s = slice(q * CH, (q + 1) * CH)
                                last = nc.vector.scalar_tensor_tensor(
                                    out=xa[:, b % 2, s], in0=bank[2][:, s], scalar=rstd2[:, b, 1, q:q + 1],
                                    in1=xp[:, b % 2, s], op0=ALU.mult, op1=ALU.add)
                            last.then_inc(xa_ready, 1)
                        b = j + 2
                        if n == 6 and 0 <= b < NB:
                            dve.wait_ge(rstd2_ready, b + 1)
                            if b >= 2:
                                dve.wait_ge(xp_t_done, b - 1)
                            normalise(xp, h, b, mv2, rstd2).then_inc(xp_ready, 1)

            @block.tensor
            def _(pe):
                mm = nc.tensor.matmul

                def prepare(t):
                    if t >= 2:
                        pe.wait_ge(prep_ready, t - 1)
                    dst = bank[4 + t % 2]
                    if t < N_POW:
                        out_, lhs, rhs, need = prep[t]
                        if need > max(t - 1, 0):
                            pe.wait_ge(prep_ready, need)
                        last = mm(dst[:, 0:out_.shape[1]], lhs, rhs, start=True, stop=True)
                    else:
                        pe.wait_ge(ld_pb, 16)
                        mm(dst[:, 0:1], pb[:, PB["attn"]], pa[:, PA["ln_b"]], start=True, stop=True)
                        last = mm(dst[:, 1:1 + NE], pb[:, PB["nw"]], pa[:, PA["fc2_b"]], start=True, stop=True)
                    last.then_inc(prep_done, 1)

                def fuse(e):
                    pe.wait_ge(ld_fc2, 16)
                    if e == 0:
                        pe.wait_ge(x2_ready[0], T)
                    else:
                        pe.wait_ge(fused_ready, e)
                    for c in range(HC):
                        last = mm(bank[5][:, c * CH:(c + 1) * CH], fc2_w[:, e * HID + c * P:e * HID + (c + 1) * P],
                                  pb[:, PB["nw"]], start=True, stop=True)
                    last.then_inc(fused_done, 1)

                def spread_ids(b):
                    for s in range(2):
                        n = 2 * b + s
                        if n >= 2:
                            pe.wait_ge(oh_ready, n - 1)
                        mm(bank[n % 2][:, 0:EXT * NCH // 2], rowsel[:, n, :], ids_b[:], start=True,
                           stop=True).then_inc(idb_done, 1)

                def gather(b):
                    pe.wait_ge(oh_ready, 2 * b + 2)
                    if b >= 1:
                        pe.wait_ge(h_ready, b)
                    for q in range(NQ):
                        for n, (tap, part) in enumerate([(0, 0), (0, 1), (1, 0), (1, 1)]):
                            at = (q * TQ + tap) * NCH
                            last = mm(bank[2][:, q * CH:(q + 1) * CH], onehot[:, b % 2, at:at + P], tab[:, part, tap, :],
                                      start=(n == 0), stop=(n == 3))
                    last.then_inc(gat_done, 1)

                def transpose_u(b):
                    pe.wait_ge(u_ready, b + 1)
                    pe.wait_ge(u_act_ready, b + 1)
                    if b >= 1:
                        pe.wait_ge(uT_ready, b)
                    for q in range(NQ):
                        s = slice(q * CH, (q + 1) * CH)
                        last = nc.tensor.transpose(bank[3][:, s], u[:, b % 2, s], ident)
                    last.then_inc(u_t_done, 1)

                def scan_step(g, i):
                    dst = bank[6 + i % 2]
                    if i == 0:
                        pe.wait_ge(uT_ready, GB * (g + 1))
                    if g == 1 and i < 2:
                        pe.wait_ge(x_ready[0], T - 1 + i)
                    if i >= 2:
                        pe.wait_ge(x_ready[g], i - 1)
                    w = GB * NCH
                    for a in range(NP):
                        last = mm(dst[:, a * w:(a + 1) * w], pa[:, PA["b"]][:, a * P:(a + 1) * P], uT[:, g * GB:(g + 1) * GB, i, :],
                                  start=(a == 0), stop=(i == 0 and a == NP - 1))
                    if i >= 1:
                        pe.wait_ge(x_ready[g], i)
                        last = mm(dst[:, 0:NP * w], a1, x_step(g, i - 1), start=False, stop=True)
                    last.then_inc(step_done[g], 1)

                def ks_step(g, lv):
                    if lv == 0:
                        pe.wait_ge(init_ready, NG * NP)
                        pe.wait_ge(ends_ready[g], 1)
                        pe.wait_ge(prep_ready, N_POW)
                        pe.wait_ge(h_ready, NB)
                        pe.wait_ge(uT_ready, NB)
                    else:
                        pe.wait_ge(ks_ready[g], lv)
                    mm(ks_bank(g, lv), step_of(lv), ks_src(g, lv), start=True, stop=True).then_inc(ks_done[g], 1)

                def second_pass(g, i):
                    if i == 0:
                        pe.wait_ge(ks_ready[g], LEVELS)
                        pe.wait_ge(prep_ready, N_PREP)
                        pe.wait_ge(x_ready[g], T)
                    if i >= len(P2_BANKS[g]):
                        pe.wait_ge((x2_ready[0], corr_ready)[g], i + 1 - len(P2_BANKS[g]))
                    mm(second_bank(g, i), a1 if i == 0 else pw[:, i + 1, :],
                       E[:, g, :, :].rearrange("p a k -> p (a k)"), start=True, stop=True).then_inc(p2_done[g], 1)

                pe.wait_ge(ld_pc, 16)
                pe.wait_ge(amax_e_ready, 1)
                nc.tensor.transpose(bank[6][0:1, 0:VOC], amax_e[:], ident[0:VOC, 0:VOC]).then_inc(amax_t_done, 1)
                pe.wait_ge(pool_const, 2)
                pe.wait_ge(amax_row_ready, 1)
                mm(bank[7][:, 0:1], ones1[:], amax_row[:], start=True, stop=True).then_inc(amax_bc_done, 1)
                pe.wait_ge(ids_ready, 1)
                spread_ids(0)
                pe.wait_ge(ld_pa, 32)
                prepared = 0
                for b in range(NB + 2):
                    if b + 1 < NB:
                        spread_ids(b + 1)
                    if b == 0:
                        pe.wait_ge(tab_ready, 1)
                    if b < NB:
                        gather(b)
                    if b >= 2:
                        transpose_u(b - 2)
                    for t in range(2 * b, min(2 * b + 2, N_POW)):
                        prepare(t)
                        prepared = t + 1
                    for i in embed_round_steps(b):
                        scan_step(0, i)
                for i in range(G0_FRONT, T):
                    scan_step(0, i)
                    for t in range(prepared, min(prepared + 2, N_PREP)):
                        prepare(t)
                        prepared = t + 1
                for lv in range(LEVELS):
                    ks_step(0, lv)
                    scan_step(1, lv)
                    if prepared < N_PREP:
                        prepare(prepared)
                        prepared += 1
                assert prepared == N_PREP
                for i in range(T):
                    second_pass(0, i)
                    if i % 2 == 0:
                        scan_step(1, LEVELS + i // 2)

                def transpose_x(b):
                    g, bb = divmod(b, GB)
                    pe.wait_ge(x2_ready[g], T)
                    for a in range(NP):
                        if b >= 1:
                            pe.wait_ge(xh_ready, 2 * (b - 1) + a + 1)
                        for q in range(NQ):
                            last = nc.tensor.transpose(bank[a][:, q * P:(q + 1) * P],
                                                       X[:, g, a * GB + bb, q * TQ:(q + 1) * TQ, :].rearrange("p i k -> p (i k)"),
                                                       ident)
                        last.then_inc(xt_done, 1)

                def transpose_r(b):
                    pe.wait_ge(rs_ready, b + 1)
                    if b == 0:
                        pe.wait_ge(x2_ready[0], T)
                    if b >= 4:
                        pe.wait_ge(res_ready, b - 3)
                    nc.tensor.transpose(bank_rt, r_s[:, b % 2, :, :].rearrange("p s n -> p (s n)"),
                                        ident).then_inc(rt_done, 1)

                def spread_r(b):
                    pe.wait_ge(rT_ready, b + 1)
                    pe.wait_ge(sel_ready, 1)
                    pe.wait_ge(amax_ready, b + 1)
                    for a in range(NP):
                        for q in range(NQ):
                            n = q * NP + a
                            last = mm(bank[a][:, q * P:(q + 1) * P], sel_r[:, n * P:(n + 1) * P], r_T[:, b % 2, :],
                                      start=True, stop=True)
                        last.then_inc(R_done, 1)

                def mixer_out(b, q):
                    if q == 0:
                        pe.wait_ge(xh_ready, 2 * b + 2)
                        pe.wait_ge(ks_ready[0], LEVELS)
                        if b >= 2:
                            pe.wait_ge(xa_ready, b - 1)
                    dst = bank[2][:, q * CH:(q + 1) * CH]
                    mm(dst, uT[:, b, q * TQ:(q + 1) * TQ, :].rearrange("p i k -> p (i k)"), pb[:, PB["d"]],
                       start=True, stop=False)
                    for a in range(NP):
                        last = mm(dst, xh[:, b % 2, a, q * P:(q + 1) * P], pb[:, PB["c"]][:, a * CH:(a + 1) * CH],
                                  start=False, stop=(a == NP - 1))
                    if q == NQ - 1:
                        last.then_inc(y_done, 1)

                def transpose_xp(b):
                    pe.wait_ge(xp_ready, b + 1)
                    if b == 0:
                        pe.wait_ge(ks_ready[1], LEVELS)
                    else:
                        pe.wait_ge(xaT_ready, b)
                    for q in range(NQ):
                        s = slice(q * CH, (q + 1) * CH)
                        last = nc.tensor.transpose(bank[3][:, s], xp[:, b % 2, s], ident)
                    last.then_inc(xp_t_done, 1)

                def attn(b):
                    pe.wait_ge(attn_g_ready, 1)
                    pe.wait_ge(xpT_ready, b + 1)
                    pe.wait_ge(h2_ready, min(b + 2, NB))
                    for q in range(NQ):
                        s = slice(q * CH, (q + 1) * CH)
                        last = mm(bank[2][:, s], xpT[:, b % 2, s], attn_g[:], start=True, stop=True)
                    last.then_inc(attn_done, 1)

                def transpose_xa(b):
                    pe.wait_ge(xa_ready, b + 1)
                    for q in range(NQ):
                        s = slice(q * CH, (q + 1) * CH)
                        last = nc.tensor.transpose(bank[3][:, s], xa[:, b % 2, s], ident)
                    last.then_inc(xa_t_done, 1)

                def fc1_part(b, n):
                    half, c = divmod(n, HC)
                    e = expert(b, half)
                    if n == 0:
                        pe.wait_ge(xaT_ready, b + 1)
                        if b == 0:
                            pe.wait_ge(ld_fc1, 16)
                            pe.wait_ge(corr_ready, T)
                            pe.wait_ge(fused_ready, NE)
                    if 8 * b + n >= 2:
                        pe.wait_ge(hid_ready, 8 * b + n - 1)
                    mm(bank[5 + n % 2][:, 0:HALF], fc1_w[:, e * HID + c * P:e * HID + (c + 1) * P],
                       xaT[:, b % 2, half, :], start=True, stop=True).then_inc(fc1_done, 1)

                def out_part(b, n):
                    half, c = divmod(n, HC)
                    e = expert(b, half)
                    if n == 0 and b >= 1:
                        pe.wait_ge(gel_ready, b)
                    pe.wait_ge(hid_ready, 8 * b + n + 1)
                    last = mm(bank[7][:, half * HALF:(half + 1) * HALF], out_w[:, e, c, :], hid[:, half, c, :],
                              start=(c == 0), stop=(c == HC - 1))
                    if c == HC - 1:
                        last.then_inc(o_done, 1)

                def transpose_h(b):
                    pe.wait_ge(rT_ready, min(b + 4, NB))
                    if b >= 1:
                        pe.wait_ge(res_ready, b)
                    for q in range(NQ):
                        s = slice(q * CH, (q + 1) * CH)
                        last = nc.tensor.transpose(bank[4][:, s], h[:, b, s], ident)
                    last.then_inc(h2_t_done, 1)

                for j in range(-3, NB):
                    for n in range(8):
                        if n == 0 and 0 <= j + 1 < NB:
                            transpose_xp(j + 1)
                        if j < 0:
                            what, i = group1_at(j, n)
                            {"step": scan_step, "doubling": ks_step, "second": second_pass}[what](1, i)
                            if fused_at(j, n) is not None:
                                fuse(fused_at(j, n))
                        else:
                            fc1_part(j, n)
                            if n >= 2:
                                out_part(j, n - 2)
                        if n in (1, 2) and 0 <= j + 2 < NB:
                            mixer_out(j + 2, 2 * (n - 1))
                            mixer_out(j + 2, 2 * (n - 1) + 1)
                        if n == max_slot(j) and j + 3 < NB:
                            transpose_x(j + 3)
                        if n == 5 and 0 <= j + 1 < NB:
                            attn(j + 1)
                        if n == 7 and 0 <= j + 1 < NB:
                            transpose_xa(j + 1)
                        if n == 7 and j + 3 < NB:
                            transpose_r(j + 3)
                    if j >= 0:
                        out_part(j, 6)
                        out_part(j, 7)
                    if j + 3 < NB:
                        spread_r(j + 3)
                    if j >= 0:
                        transpose_h(j)


def kernel(x, L0_tok_emb_weight, L0_tok_conv_weight, L0_attn_init_states, L0_attn_A, L0_attn_B, L0_attn_C,
           L0_attn_D, L0_ffn_ln_g, L0_ffn_ln_b, L0_ffn_attn_w, L0_ffn_attn_b, L0_ffn_gate_w, L0_ffn_fc1_w,
           L0_ffn_fc1_b, L0_ffn_fc2_w, L0_ffn_fc2_b, L0_ffn_next_w, L0_ffn_next_b):
    import concourse.bacc as bacc
    from concourse.bass_utils import run_bass_kernel_spmd
    import ml_dtypes

    f = lambda a: np.asarray(a)
    ids = f(x).reshape(NB, NCH, T).transpose(0, 2, 1)
    before = np.full((NB, 1, NCH), -1, ids.dtype)
    before[:, 0, 1:] = ids[:, T - 1, :-1]
    ids = np.concatenate([before, ids], 1).reshape(2 * NB, EXT * NCH // 2)

    def diag(a):
        out = np.zeros((P, P), a.dtype)
        out[:DH, :DH] = a
        out[DH:, DH:] = a
        return out

    A = f(L0_attn_A)
    parts = dict(
        a=diag(A), at=diag(A.T), b=f(L0_attn_B),
        init=f(L0_attn_init_states).reshape(NP, P).T, ln_g=f(L0_ffn_ln_g)[:, None], ln_b=f(L0_ffn_ln_b)[:, None],
        attn_b=f(L0_ffn_attn_b)[:, None], next_b=f(L0_ffn_next_b)[:, None],
        fc1_b=f(L0_ffn_fc1_b).reshape(NE * HC, P).T, fc2_b=f(L0_ffn_fc2_b).T)
    pack_a = np.concatenate([parts[n] for n in PA_COLS], 1)
    parts = dict(nw=f(L0_ffn_next_w).T, c=f(L0_attn_C).reshape(NP, P, CH).transpose(1, 0, 2).reshape(P, NP * CH),
                 d=f(L0_attn_D), attn=f(L0_ffn_attn_w).T)
    pack_b = np.concatenate([parts[n] for n in PB_COLS], 1)
    pack_c = np.concatenate([np.eye(P, dtype=np.float32), np.arange(P, dtype=np.float32)[:, None]], 1)
    sel = np.zeros((NS, NQ, NH, NQ, NP, 2, DH), np.float32)
    for q in range(NQ):
        for n in range(NH):
            sel[:, q, n, q, n // 2, n % 2, :] = 1
    arrays = dict(
        ids=ids, emb=f(L0_tok_emb_weight), conv=f(L0_tok_conv_weight)[:, 0, :].T.reshape(1, 2 * CH),
        pack_a=pack_a, pack_b=pack_b, sel=sel.reshape(NS * NQ * NH, NQ * NP * P),
        pack_c=pack_c, rows=np.repeat(np.eye(2 * NB, dtype=ml_dtypes.bfloat16), P, 1),
        fc1=f(L0_ffn_fc1_w).transpose(2, 0, 1).reshape(P, NE * HID),
        fc2=f(L0_ffn_fc2_w).transpose(1, 0, 2))
    arrays = {n: np.ascontiguousarray(a) for n, a in arrays.items()}
    nc = bacc.Bacc("TRN2", target_bir_lowering=False, num_devices=1)
    args = {n: nc.dram_tensor(f"in_{n}", a.shape, mybir.dt.from_np(a.dtype), kind="ExternalInput").ap()
            for n, a in arrays.items()}
    out = nc.dram_tensor("out", (NB, P, L), F32, kind="ExternalOutput").ap()
    build(nc, out=out, **args)
    r = run_bass_kernel_spmd(nc, [{f"in_{n}": a for n, a in arrays.items()}], core_ids=[0])
    got = r.results[0]["out"].reshape(NB, CH, 2, T, NCH // 2)
    return np.ascontiguousarray(got.transpose(0, 2, 4, 3, 1)).reshape(NB, L, CH)
```

```python
from contextlib import ExitStack

import concourse.bass as bass
import numpy as np
from concourse import mybir

ALU = mybir.AluOpType
ACT = mybir.ActivationFunctionType
AX = mybir.AxisListType
F32 = mybir.dt.float32
BF16 = mybir.dt.bfloat16
F32R = mybir.dt.float32r
I32 = mybir.dt.int32

P = 128
NB = 8
L = 512
T = 16
NCH = L // T
NG = 2
GB = NB // NG
VOC = 125
NH, DH = 4, 64
NP = NH * DH // P
CH = 128
NE, HID = 8, 512
HC = HID // P
TQ = P // NCH
NQ = T // TQ
EXT = T + 1
HALF = L // 2
QMAX = 127.0
EPS = 1e-5
ROUND = 12582912.0
E2 = float(np.exp(np.float32(2.0)))
NS = 2
LEVELS = NCH.bit_length() - 1
HID_SLOTS = 4
CORR_SLOTS = 4
DVE_ROUND = NB - 2
HT_SLOTS = 4
LAG = 4

PA_COLS = dict(a=P, at=P, b=NP * P, init=NP, ln_g=1, ln_b=1, attn_b=1, next_b=1,
               fc1_b=NE * HC, fc2_b=NE)
PC_COLS = dict(ident=P, iota=1, tile=NQ)
PB_COLS = dict(nw=CH, c=NP * CH, d=CH, attn=CH)


def spans(cols):
    out, at = {}, 0
    for name, n in cols.items():
        out[name] = slice(at, at + n)
        at += n
    return out, at


PA, PA_N = spans(PA_COLS)
PB, PB_N = spans(PB_COLS)
PC, PC_N = spans(PC_COLS)


def build(nc, ids, rows, emb, conv, pack_a, pack_b, pack_c, sel, fc1, fc2, out):
    with ExitStack() as ctx:
        def sb(name, shape, dt=F32):
            return ctx.enter_context(nc.sbuf_tensor(name, shape, dt))

        def sem(name):
            return ctx.enter_context(nc.semaphore(name))

        pa = sb("pa", [P, PA_N])
        pc = sb("pc", [P, PC_N])
        pb = sb("pb", [P, PB_N])
        sel_r = sb("sel_r", [NS * NQ * NH, NP * P], F32R)
        fc1_p = [sb(f"fc1_p{s}", [P, NE * HID], F32R) for s in range(NS)]
        out_hi = sb("out_hi", [P, NE, HC * CH], F32R)
        with ExitStack() as embedding:
            def sb_embedding(name, shape, dt=F32):
                return embedding.enter_context(nc.sbuf_tensor(name, shape, dt))

            emb_w = sb_embedding("emb_w", [VOC, CH])
            conv_w = sb_embedding("conv_w", [P, 2 * CH])
            q_e = sb_embedding("q_e", [VOC, CH])
            q_c = sb_embedding("q_c", [P, 2 * CH])
            prod = sb_embedding("prod", [VOC, 2, CH])
            tab = sb_embedding("tab", [VOC, 2, 2, CH], BF16)
            onehot = sb_embedding("onehot", [VOC, 2, EXT * NCH], BF16)
            st1 = sb_embedding("st1", [P, 2, NQ, 6])
            tmp1 = sb_embedding("tmp1", [P, 2, NQ])
            u = sb_embedding("u", [P, 2, NQ * CH])
        out_p = [out_hi, sb("out_lo", [P, NE, HC * CH], F32R)]
        ones1 = sb("ones1", [1, P])
        neg_half = sb("neg_half", [P, 2 * NQ])
        inv_e = sb("inv_e", [P, 1])
        inv_c = sb("inv_c", [P, 1])
        warm = sb("warm", [1, 1])
        amax_e = sb("amax_e", [VOC, 1])
        amax_row = sb("amax_row", [1, 1])
        scale_e = sb("scale_e", [P, 1])
        scale_c = sb("scale_c", [P, 1])
        scale_h = sb("scale_h", [P, 1])
        h = sb("h", [P, NB, NQ * CH])
        mv1 = sb("mv1", [P, NB, NQ, 2])
        rstd1 = sb("rstd1", [P, NB, NQ])
        shift1 = sb("shift1", [P, NB, NQ])
        uT = sb("uT", [P, NB, T, NCH])
        with ExitStack() as scan_only:
            def sb_scan(name, shape):
                return scan_only.enter_context(nc.sbuf_tensor(name, shape, F32))

            pw = sb_scan("pw", [P, T + 1, P])
            pw_t = sb_scan("pw_t", [P, T.bit_length(), P])
            pk = sb_scan("pk", [P, LEVELS, P])
            pk_t = sb_scan("pk_t", [P, LEVELS, P])
        gel = sb("gel", [P, 2, L])
        res = sb("res", [P, 2, L])
        hid_f = sb("hid_f", [P, HID_SLOTS, HALF])
        sb("spare", [P, (T + 1 + T.bit_length() + 2 * LEVELS) * P - 4 * L - HID_SLOTS * HALF])
        attn_m = sb("attn_m", [P, CH])
        attn_c = sb("attn_c", [P, 1])
        out_c = sb("out_c", [P, NE])
        X = sb("X", [P, NG, NP * GB, T, NCH])
        corr = sb("corr", [P, CORR_SLOTS, NP * GB, NCH])
        E = sb("E", [P, NG, NP * GB, NCH])
        amax = sb("amax", [P, 2, NQ, NH])
        rcp = sb("rcp", [P, 2, NQ * NH])
        r_s = sb("r_s", [P, 2, NS, NQ * NH])
        r_T = sb("r_T", [NS * NQ * NH, 2, L], F32R)
        st2 = sb("st2", [P, 2, NQ, 6])
        mv2 = sb("mv2", [P, NB, NQ, 2])
        spread2 = sb("spread2", [P, 2, 2, NQ])
        rstd2 = sb("rstd2", [P, NB, 2, NQ])
        with ExitStack() as early:
            def sb_early(name, shape, dt=F32):
                return early.enter_context(nc.sbuf_tensor(name, shape, dt))

            fc2_w = sb_early("fc2_w", [P, NE * HID])
            fc1_w = sb_early("fc1_w", [P, NE * HID])
            ids_i = sb_early("ids_i", [2 * NB, EXT * NCH // 2], I32)
            ids_b = sb_early("ids_b", [2 * NB, EXT * NCH // 2], BF16)
            rowsel = sb_early("rowsel", [2 * NB, 2 * NB, P], BF16)
            centre = sb_early("centre", [P, P])
            attn_g = sb_early("attn_g", [P, CH])
            sel_f = sb_early("sel_f", [NS * NQ * NH, NP * P])
        hid_p = [sb(f"hid_p{s}", [P, 2, HC, HALF], F32R) for s in range(NS)]
        xh = sb("xh", [P, 2, NP, L])
        xp = sb("xp", [P, NQ * CH])
        hT = sb("hT", [P, HT_SLOTS, L])
        xa = sb("xa", [P, NQ * CH])
        xaT_p = [sb(f"xaT_p{s}", [P, 2, 2, HALF], F32R) for s in range(NS)]
        bank = [ctx.enter_context(nc.psum_tensor(f"bank{n}", [P, 512], F32)) for n in range(8)]
        bank_rt = bank[4][0:NS * NQ * NH, 0:P]

        ident = pc[:, PC["ident"]]

        ld_ids, ld_emb, ld_pa, ld_pb = sem("ld_ids"), sem("ld_emb"), sem("ld_pa"), sem("ld_pb")
        ld_pc, ld_sel, ld_fc1, ld_fc2 = sem("ld_pc"), sem("ld_sel"), sem("ld_fc1"), sem("ld_fc2")
        sel_ready, v2_ready, ld_conv = sem("sel_ready"), sem("v2_ready"), sem("ld_conv")
        pool_const = sem("pool_const")
        pool_link, dve_link = sem("pool_link"), sem("dve_link")
        ids_ready, amax_e_ready, amax_row_ready, tab_ready = (
            sem("ids_ready"), sem("amax_e_ready"), sem("amax_row_ready"), sem("tab_ready"))
        attn_g_ready, scale_c_ready, q_c_ready = sem("attn_g_ready"), sem("scale_c_ready"), sem("q_c_ready")
        amax_t_done, amax_bc_done = sem("amax_t_done"), sem("amax_bc_done")
        idb_done, oh_ready, gat_done, h_ready = sem("idb_done"), sem("oh_ready"), sem("gat_done"), sem("h_ready")
        st1_ready, mv1_ready, rstd1_ready, u_ready = (
            sem("st1_ready"), sem("mv1_ready"), sem("rstd1_ready"), sem("u_ready"))
        u_act_ready = sem("u_act_ready")
        u_t_done, uT_ready = sem("u_t_done"), sem("uT_ready")
        prep_done, prep_ready = sem("prep_done"), sem("prep_ready")
        step_done, x_ready = [sem(f"step_done{g}") for g in range(NG)], [sem(f"x_ready{g}") for g in range(NG)]
        fused_done, fused_ready, corr_ready = sem("fused_done"), sem("fused_ready"), sem("corr_ready")
        init_ready, ends_ready = sem("init_ready"), [sem(f"ends_ready{g}") for g in range(NG)]
        ks_done, ks_ready = [sem(f"ks_done{g}") for g in range(NG)], [sem(f"ks_ready{g}") for g in range(NG)]
        p2_done, x2_ready = [sem(f"p2_done{g}") for g in range(NG)], [sem(f"x2_ready{g}") for g in range(NG)]
        ks_copied, full_ready = sem("ks_copied"), sem("full_ready")
        xt_done, amax_ready, rs_ready = sem("xt_done"), sem("amax_ready"), sem("rs_ready")
        rt_done, rT_ready, R_done, xh_ready = sem("rt_done"), sem("rT_ready"), sem("R_done"), sem("xh_ready")
        y_done, h2_ready, st2_ready, mv2_ready = sem("y_done"), sem("h2_ready"), sem("st2_ready"), sem("mv2_ready")
        rstd2_ready, xp_ready = sem("rstd2_ready"), sem("xp_ready")
        centre_ready = sem("centre_ready")
        h_t_done, hT_ready, attn_done, xa_ready = (
            sem("h_t_done"), sem("hT_ready"), sem("attn_done"), sem("xa_ready"))
        xa_t_done, xaT_ready = sem("xa_t_done"), sem("xaT_ready")
        fc1_done, hid_ready, o_done, gel_ready = sem("fc1_done"), sem("hid_ready"), sem("o_done"), sem("gel_ready")
        hid_lo_dve = sem("hid_lo_dve")
        fc1_split, fused_lo_ready, xaT_lo_ready, hid_lo_ready = (
            sem("fc1_split"), sem("fused_lo_ready"), sem("xaT_lo_ready"), sem("hid_lo_ready"))
        res_ready = sem("res_ready")
        stored = [sem("stored0"), sem("stored1")]

        def powers(n0, n1):
            return pw[:, n0:n1 + 1, :].rearrange("p n m -> p (n m)")

        a1, a1t = pa[:, PA["a"]], pa[:, PA["at"]]
        prep = [
            (powers(2, 2), a1t, a1, 0), (pw_t[:, 1, :], a1, a1t, 0),
            (pw[:, 3, :], pw_t[:, 1, :], a1, 2), (pw[:, 4, :], pw_t[:, 1, :], pw[:, 2, :], 2),
            (pw_t[:, 2, :], pw[:, 2, :], pw_t[:, 1, :], 2),
            (powers(5, 8), pw_t[:, 2, :], powers(1, 4), 5), (pw_t[:, 3, :], pw[:, 4, :], pw_t[:, 2, :], 5),
            (powers(9, 12), pw_t[:, 3, :], powers(1, 4), 7), (powers(13, 16), pw_t[:, 3, :], powers(5, 8), 7),
            (pw_t[:, 4, :], pw[:, 8, :], pw_t[:, 3, :], 7),
        ]
        prev, prev_t = pw[:, T, :], pw_t[:, 4, :]
        for lv in range(1, LEVELS):
            need = len(prep)
            prep.append((pk[:, lv, :], prev_t, prev, need))
            if lv < LEVELS - 1:
                prep.append((pk_t[:, lv, :], prev, prev_t, need))
            prev, prev_t = pk[:, lv, :], pk_t[:, lv, :]
        N_POW = len(prep)
        N_PREP = N_POW + 1
        PARTS = ((0, 0), (1, 0), (0, 1))

        def step_of(n):
            return pw[:, T, :] if n == 0 else pk[:, n, :]

        def ks_src(g, lv):
            return E[:, g, :, 0:NCH - 2 ** lv]

        def ks_dst(g, lv):
            return E[:, g, :, 2 ** lv:NCH]

        def ks_bank(g, lv):
            n = NP * GB * (NCH - 2 ** lv)
            return bank[(2, 6)[g]][:, 0:n].rearrange("p (a k) -> p a k", a=NP * GB)

        def x_step(g, i):
            return X[:, g, :, i, :]

        def expert(b, half):
            return (2 * b + half) % NE

        G0_STEPS = (0, 0, 0, 0, 0, 1, 2, 3, 4, 6)
        U_DVE = (2, 2, 2, 2, 2, 4, 4, 4)
        PREP_ROUND = ((1, 0), (1, 0), (1, 0), (1, 1), (1, 1), (1, 2), (1, 1), (1, 1), (1, 1), (1, 0))
        FUSE_STEPS = (6, 7, 8, 9, 12, 13, 14, 15)
        FUSED_FRONT = len(FUSE_STEPS) * NP // HC
        WITH_SECOND = 8
        PLAN = (
            ("step",), ("step",), ("step",), ("doubling", "fuse"), ("doubling", "fuse"), (), (), (),
            ("doubling", "fuse"), ("doubling", "fuse"), ("doubling",), (),
            ("second",), ("second",), ("second",), ("second",),
            ("second", "second"), ("second", "second"), ("second", "second"), ("second", "second"),
            ("second",), ("second",), ("second",), ("second",))

        def embed_round_steps(b):
            return range(sum(G0_STEPS[:b]), sum(G0_STEPS[:b + 1]))

        assert sum(map(sum, PREP_ROUND)) == N_POW

        def prep_tasks(b, after):
            first = sum(map(sum, PREP_ROUND[:b])) + (PREP_ROUND[b][0] if after else 0)
            return range(first, first + PREP_ROUND[b][after])

        def numbered(plan):
            done, out = dict(step=LEVELS + WITH_SECOND, doubling=0, fuse=FUSED_FRONT, second=0), []
            for names in plan:
                place = []
                for name in names:
                    place.append((name, done[name]))
                    done[name] += 1
                out.append(place)
            assert done == dict(step=T, doubling=LEVELS, fuse=NE, second=T)
            return out

        plan = numbered(PLAN)

        def scan_work(j, n):
            return plan[8 * (j + 3) + n]

        P2_BANKS = ((4, 5, 0, 1), (6, 7))

        def fuse_bank(e):
            return bank[(0 if e < FUSED_FRONT else 4) + e % 2]

        def second_bank(g, i):
            return bank[P2_BANKS[g][i % len(P2_BANKS[g])]][:, 0:NP * GB * NCH]

        def out_bank(b, half):
            if b == NB - 1:
                return bank[half]
            return bank[0 if b == NB - 3 else 7]

        def wait_low(engine, part):
            k = part - 8 * DVE_ROUND
            if k < 0:
                engine.wait_ge(hid_lo_ready, part + 1)
            elif k % 2 == 0:
                engine.wait_ge(hid_lo_ready, 8 * DVE_ROUND + k // 2 + 1)
            else:
                engine.wait_ge(hid_lo_dve, k // 2 + 1)

        with nc.Block() as block:

            @block.sync
            def _(sp):
                sp.dma_start(emb_w[:], emb).then_inc(ld_emb, 16)
                sp.dma_start(ids_i[:], ids).then_inc(ld_ids, 16)
                sp.dma_start(rowsel[:].rearrange("r j p -> r (j p)"), rows).then_inc(ld_ids, 16)
                sp.dma_start(pa[:], pack_a).then_inc(ld_pa, 16)
                sp.dma_start(pw[:, 1, :], pack_a[:, PA["a"]]).then_inc(ld_pa, 16)
                sp.dma_start(pb[:], pack_b).then_inc(ld_pb, 16)
                sp.dma_start(fc2_w[:].rearrange("p (e m) -> p e m", e=NE), fc2).then_inc(ld_fc2, 16)
                sp.dma_start(sel_f[:], sel).then_inc(ld_sel, 16)
                sp.dma_start(fc1_w[:], fc1).then_inc(ld_fc1, 16)
                for b in range(NB - 1):
                    sp.wait_ge(res_ready, b + 1)
                    sp.dma_start(out[b], res[:, b % 2, :]).then_inc(stored[b % 2], 16)
                for half in range(2):
                    b, s = NB - 1, slice(half * HALF, (half + 1) * HALF)
                    sp.wait_ge(res_ready, NB + half)
                    sp.dma_start(out[b][:, s], res[:, b % 2, s]).then_inc(stored[b % 2], 16)
                sp.wait_ge(stored[0], 16 * (NB // 2))
                sp.wait_ge(stored[1], 16 * (NB // 2 + 1))

            @block.gpsimd
            def _(pool):
                nc.gpsimd.memset(ones1[:], 1.0).then_inc(pool_const, 1)
                nc.gpsimd.memset(neg_half[:], -0.5).then_inc(pool_const, 1)
                link = [0]

                def chained(ins):
                    link[0] += 1
                    ins.then_inc(pool_link, 1)
                    pool.wait_ge(pool_link, link[0])

                pool.wait_ge(pool_const, 2)
                pool.wait_ge(ld_pa, 32)
                for g in range(NG):
                    for a in range(NP):
                        nc.gpsimd.tensor_copy(E[:, g, a * GB:(a + 1) * GB, 0],
                                              pa[:, PA["init"]][:, a:a + 1].broadcast_to([P, GB])).then_inc(init_ready, 1)
                for b in range(NB):
                    pool.wait_ge(mv1_ready, b + 1)
                    r = rstd1[:, b, :]
                    chained(nc.gpsimd.tensor_scalar(tmp1[:, 0, :], mv1[:, b, :, 1], EPS, None, ALU.add))
                    chained(nc.gpsimd.tensor_tensor(r, tmp1[:, 0, :], neg_half[:, 0:NQ], ALU.pow))
                    chained(nc.gpsimd.tensor_tensor(tmp1[:, 1, :], mv1[:, b, :, 0], r, ALU.mult))
                    nc.gpsimd.tensor_scalar(shift1[:, b, :], tmp1[:, 1, :], -1.0, None, ALU.mult).then_inc(rstd1_ready, 1)
                pool.wait_ge(ld_sel, 16)
                nc.gpsimd.tensor_copy(sel_r[:], sel_f[:]).then_inc(sel_ready, 1)
                for e in range(NE):
                    if e == 0:
                        pool.wait_ge(ld_fc1, 16)
                    s = slice(e * HID, (e + 1) * HID)
                    chained(nc.gpsimd.tensor_copy(fc1_p[0][:, s], fc1_w[:, s]))
                    nc.gpsimd.tensor_tensor(fc1_p[1][:, s], fc1_w[:, s], fc1_p[0][:, s].bitcast(F32),
                                            ALU.subtract).then_inc(fc1_split, 1)

                for j in range(-3, NB):
                    for n in range(8):
                        if 0 <= j < DVE_ROUND or (j >= DVE_ROUND and n % 2 == 0):
                            m, (half, c) = 8 * j + n, divmod(n, HC)
                            pool.wait_ge(hid_ready, m + 1)
                            if j >= 1:
                                pool.wait_ge(o_done, 2 * (j - 1) + half + 1)
                            nc.gpsimd.tensor_tensor(hid_p[1][:, half, c, :], hid_f[:, m % HID_SLOTS, :],
                                                    hid_p[0][:, half, c, :].bitcast(F32),
                                                    ALU.subtract).then_inc(hid_lo_ready, 1)
                        if j < 0:
                            for what, i in scan_work(j, n):
                                if what == "doubling":
                                    pool.wait_ge(ks_copied, i + 1)
                                    nc.gpsimd.tensor_tensor(ks_dst(1, i), ks_dst(1, i), corr[:, i % 2, :, 2 ** i:NCH],
                                                            ALU.add).then_inc(ks_ready[1], 1)
                                if what == "second":
                                    pool.wait_ge(corr_ready, i + 1)
                                    nc.gpsimd.tensor_tensor(x_step(1, i), x_step(1, i), corr[:, i % CORR_SLOTS],
                                                            ALU.add).then_inc(x2_ready[1], 1)
                        b = j + 2
                        if n == 3 and 0 <= b < NB:
                            pool.wait_ge(v2_ready, b + 1)
                            nc.gpsimd.tensor_tensor(rstd2[:, b, :, :].rearrange("p s q -> p (s q)"),
                                                    spread2[:, b % 2, :, :].rearrange("p s q -> p (s q)"), neg_half[:],
                                                    ALU.pow).then_inc(rstd2_ready, 1)

            @block.scalar
            def _(act):
                act.dma_start(conv_w[:], conv[0:1, :].broadcast_to([P, 2 * CH])).then_inc(ld_conv, 16)
                act.dma_start(pc[:], pack_c).then_inc(ld_pc, 16)
                act.wait_ge(pool_const, 1)
                nc.scalar.activation(warm[:], ones1[0:1, 0:1], ACT.Gelu)

                def copy_out_prep(t):
                    act.wait_ge(prep_done, t + 1)
                    src = bank[4 + t % 2]
                    if t < N_POW:
                        dst = prep[t][0]
                        nc.scalar.activation(dst, src[:, 0:dst.shape[1]], ACT.Copy).then_inc(prep_ready, 1)
                    else:
                        nc.scalar.activation(attn_m[:], src[:, P:P + CH], ACT.Copy)
                        nc.scalar.activation(attn_c[:], src[:, 0:1], ACT.Identity, bias=pa[:, PA["attn_b"]])
                        nc.scalar.activation(out_c[:], src[:, 1:1 + NE], ACT.Identity,
                                             bias=pa[:, PA["next_b"]]).then_inc(prep_ready, 1)

                def copy_fused(e):
                    act.wait_ge(fused_done, e + 1)
                    nc.scalar.activation(out_p[0][:, e, :], fuse_bank(e)[:], ACT.Copy).then_inc(fused_ready, 1)

                def copy_step(g, i):
                    for a in range(NP):
                        act.wait_ge(step_done[g], NP * i + a + 1)
                        src = bank[6 + a][:, 0:GB * NCH].rearrange("p (b k) -> p b k", k=NCH)
                        s = slice(a * GB, (a + 1) * GB)
                        nc.scalar.activation(X[:, g, s, i, :], src, ACT.Copy).then_inc(x_ready[g], 1)
                        if i == T - 1:
                            nc.scalar.activation(E[:, g, s, 1:NCH], src[:, :, 0:NCH - 1],
                                                 ACT.Copy).then_inc(ends_ready[g], 1)

                act.wait_ge(ld_pa, 32)
                for b in range(NB + 2):
                    if b < NB:
                        act.wait_ge(gat_done, b + 1)
                        if b == 0:
                            act.wait_ge(tab_ready, 1)
                        nc.scalar.activation(h[:, b, :], bank[2][:], ACT.Relu, scale=scale_h[:]).then_inc(h_ready, 1)
                    for t in prep_tasks(b, 0):
                        copy_out_prep(t)
                    if b >= 2:
                        act.wait_ge(u_t_done, b - 1)
                        nc.scalar.activation(uT[:, b - 2, :, :].rearrange("p i k -> p (i k)"), bank[3][:],
                                             ACT.Copy).then_inc(uT_ready, 1)
                    for t in prep_tasks(b, 1):
                        copy_out_prep(t)
                    if 1 <= b <= NB and U_DVE[b - 1] < NQ:
                        act.wait_ge(rstd1_ready, b)
                        if b == 1:
                            act.wait_ge(h_ready, 1)
                        if b >= 3:
                            act.wait_ge(u_t_done, b - 2)
                        for q in range(U_DVE[b - 1], NQ):
                            s = slice(q * CH, (q + 1) * CH)
                            last = nc.scalar.activation(u[:, (b - 1) % 2, s], h[:, b - 1, s], ACT.Identity,
                                                        scale=rstd1[:, b - 1, q:q + 1], bias=shift1[:, b - 1, q:q + 1])
                        last.then_inc(u_act_ready, 1)
                    for i in embed_round_steps(b):
                        copy_step(0, i)
                copy_out_prep(N_PREP - 1)
                for lv in range(LEVELS):
                    copy_step(1, lv)
                for i in range(LEVELS, LEVELS + WITH_SECOND):
                    copy_step(1, i)

                def gelu_out(j):
                    last_batch = j == NB - 1
                    if not last_batch:
                        act.wait_ge(o_done, 2 * j + 2)
                    if j >= 2:
                        act.wait_ge(res_ready, j - 1)
                    for half in range(2):
                        if last_batch:
                            act.wait_ge(o_done, 2 * j + half + 1)
                        e = expert(j, half)
                        s = slice(half * HALF, (half + 1) * HALF)
                        last = nc.scalar.activation(gel[:, j % 2, s], out_bank(j, half)[:, s], ACT.Gelu,
                                                    bias=out_c[:, e:e + 1])
                        if last_batch or half == 1:
                            last.then_inc(gel_ready, 1)

                for j in range(-3, NB):
                    for n in range(8):
                        if j < 0:
                            for what, i in scan_work(j, n):
                                if what == "step":
                                    copy_step(1, i)
                                if what == "second":
                                    act.wait_ge(p2_done[1], i + 1)
                                    if i == 0:
                                        act.wait_ge(ks_ready[1], LEVELS)
                                    if i >= CORR_SLOTS:
                                        act.wait_ge(x2_ready[1], i + 1 - CORR_SLOTS)
                                    nc.scalar.activation(corr[:, i % CORR_SLOTS], second_bank(1, i).rearrange(
                                        "p (a k) -> p a k", k=NCH), ACT.Copy).then_inc(corr_ready, 1)
                                if what == "fuse":
                                    copy_fused(i)
                                if what == "doubling":
                                    act.wait_ge(ks_done[1], i + 1)
                                    if i >= 2:
                                        act.wait_ge(ks_ready[1], i - 1)
                                    nc.scalar.activation(corr[:, i % 2, :, 2 ** i:NCH], ks_bank(1, i),
                                                         ACT.Copy).then_inc(ks_copied, 1)
                        if n == LAG - 1 and j >= 1:
                            gelu_out(j - 1)
                        if j >= 0:
                            m, (half, c) = 8 * j + n, divmod(n, HC)
                            act.wait_ge(fc1_done, m + 1)
                            if m >= HID_SLOTS:
                                wait_low(act, m - HID_SLOTS)
                            if j >= 1:
                                act.wait_ge(o_done, 2 * (j - 1) + half + 1)
                            e = expert(j, half)
                            bias = pa[:, PA["fc1_b"]][:, e * HC + c:e * HC + c + 1]
                            src = bank[5 + n % 2][:, 0:HALF]
                            full = nc.scalar.activation(hid_f[:, m % HID_SLOTS, :], src, ACT.Gelu, bias=bias)
                            if j < DVE_ROUND:
                                nc.scalar.activation(hid_p[0][:, half, c, :], src, ACT.Gelu,
                                                     bias=bias).then_inc(hid_ready, 1)
                            else:
                                full.then_inc(full_ready, 1)
                        b = j + 3
                        if n == 2 and b < NB:
                            act.wait_ge(rt_done, b + 1)
                            if b >= 2:
                                act.wait_ge(R_done, 2 * (b - 1))
                            for q in range(NQ):
                                mask = pc[0:NS * NQ * NH, PC["tile"]][:, q:q + 1]
                                last = nc.scalar.activation(r_T[:, b % 2, q * P:(q + 1) * P], bank_rt, ACT.Copy,
                                                            scale=mask)
                            last.then_inc(rT_ready, 1)
                        b = j + 1
                        if n == 2 and 0 <= b < NB:
                            act.wait_ge(xa_t_done, b + 1)
                            if b >= 2:
                                act.wait_ge(fc1_done, 8 * (b - 1))
                            nc.scalar.activation(
                                xaT_p[0][:, b % 2, :, :].rearrange("p s (i k) -> p s i k", i=T),
                                bank[3][:].rearrange("p (i s k) -> p s i k", i=T, s=2),
                                ACT.Identity, bias=attn_c[:]).then_inc(xaT_ready, 1)
                        b = j + 2
                        if n == 5 and 0 <= b < NB:
                            act.wait_ge(h_t_done, b + 1)
                            if b >= HT_SLOTS:
                                act.wait_ge(res_ready, b + 1 - HT_SLOTS)
                            nc.scalar.activation(hT[:, b % HT_SLOTS, :], bank[4][:], ACT.Copy).then_inc(hT_ready, 1)
                gelu_out(NB - 1)

            @block.vector
            def _(dve):
                link = [0]

                def chained(ins):
                    link[0] += 1
                    ins.then_inc(dve_link, 1)
                    dve.wait_ge(dve_link, link[0])

                dve.wait_ge(ld_emb, 16)
                nc.vector.tensor_reduce(amax_e[:], emb_w[:], AX.X, ALU.max,
                                        apply_absolute_value=True).then_inc(amax_e_ready, 1)
                dve.wait_ge(ld_conv, 16)
                chained(nc.vector.tensor_reduce(scale_c[:], conv_w[:], AX.X, ALU.max, apply_absolute_value=True))
                nc.vector.tensor_scalar(scale_c[:], scale_c[:], 1.0 / QMAX, None, ALU.mult).then_inc(scale_c_ready, 1)
                dve.wait_ge(amax_t_done, 1)
                nc.vector.tensor_reduce(amax_row[:], bank[6][0:1, 0:VOC], AX.X, ALU.max).then_inc(amax_row_ready, 1)
                dve.wait_ge(scale_c_ready, 1)
                chained(nc.vector.reciprocal(inv_c[:], scale_c[:]))
                chained(nc.vector.tensor_scalar(q_c[:], conv_w[:], inv_c[:], None, ALU.mult))
                nc.vector.tensor_scalar(q_c[:], q_c[:], ROUND, -ROUND, ALU.add, ALU.add).then_inc(q_c_ready, 1)
                dve.wait_ge(ld_ids, 32)
                nc.vector.tensor_scalar(ids_b[:], ids_i[:], -1.0, float(VOC - 1), ALU.max, ALU.min).then_inc(ids_ready, 1)
                dve.wait_ge(amax_bc_done, 1)
                chained(nc.vector.tensor_scalar(scale_e[:], bank[7][:, 0:1], 1.0 / QMAX, None, ALU.mult))
                chained(nc.vector.reciprocal(inv_e[:], scale_e[:]))
                chained(nc.vector.tensor_scalar(q_e[:], emb_w[:], inv_e[0:VOC, :], None, ALU.mult))
                chained(nc.vector.tensor_scalar(q_e[:], q_e[:], ROUND, -ROUND, ALU.add, ALU.add))
                dve.wait_ge(q_c_ready, 1)
                for tap in range(2):
                    last = nc.vector.tensor_tensor(prod[:, tap, :], q_e[:], q_c[0:VOC, tap * CH:(tap + 1) * CH], ALU.mult)
                chained(last)
                chained(nc.vector.tensor_copy(tab[:, 0], prod[:]))
                nc.vector.tensor_tensor(scale_h[:], scale_e[:], scale_c[:], ALU.mult)
                nc.vector.tensor_tensor(tab[:, 1], prod[:], tab[:, 0], ALU.subtract).then_inc(tab_ready, 1)

                def one_hot(b):
                    for s in range(2):
                        n = 2 * b + s
                        dve.wait_ge(idb_done, n + 1)
                        if b >= 2:
                            dve.wait_ge(gat_done, b - 1)
                        w = EXT * NCH // 2
                        nc.vector.tensor_scalar(onehot[:, b % 2, s * w:(s + 1) * w], bank[n % 2][0:VOC, 0:w],
                                                pc[0:VOC, PC["iota"]], None, ALU.is_equal).then_inc(oh_ready, 1)

                def statistics(b, st, st_ready, mv, mv_ready):
                    for q in range(NQ):
                        last = nc.vector.bn_stats(st[:, b % 2, q, :], h[:, b, q * CH:(q + 1) * CH])
                    last.then_inc(st_ready, 1)
                    dve.wait_ge(st_ready, b + 1)
                    for q in range(NQ):
                        last = nc.vector.bn_aggr(mv[:, b, q, :], st[:, b % 2, q, :])
                    last.then_inc(mv_ready, 1)

                dve.wait_ge(ld_pc, 16)
                one_hot(0)
                one_hot(1)
                for b in range(NB + 1):
                    if b + 2 < NB:
                        one_hot(b + 2)
                    if b < NB:
                        dve.wait_ge(h_ready, b + 1)
                        statistics(b, st1, st1_ready, mv1, mv1_ready)
                    if b >= 1:
                        dve.wait_ge(rstd1_ready, b)
                        if b >= 3:
                            dve.wait_ge(u_t_done, b - 2)
                        for q in range(U_DVE[b - 1]):
                            s = slice(q * CH, (q + 1) * CH)
                            last = nc.vector.tensor_scalar(u[:, (b - 1) % 2, s], h[:, b - 1, s],
                                                           mv1[:, b - 1, q, 0:1], rstd1[:, b - 1, q:q + 1],
                                                           ALU.subtract, ALU.mult)
                        last.then_inc(u_ready, 1)
                dve.wait_ge(ld_pb, 16)
                dve.wait_ge(ld_pa, 32)
                nc.vector.tensor_scalar(attn_g[:], pb[:, PB["attn"]], pa[:, PA["ln_g"]], None,
                                        ALU.mult).then_inc(attn_g_ready, 1)
                dve.wait_ge(ld_pc, 16)
                nc.vector.tensor_scalar(centre[:], ident, -1.0 / CH, None, ALU.add).then_inc(centre_ready, 1)

                def ks_add(lv):
                    dve.wait_ge(ks_done[0], lv + 1)
                    nc.vector.tensor_tensor(ks_dst(0, lv), ks_dst(0, lv), ks_bank(0, lv), ALU.add).then_inc(ks_ready[0], 1)

                def p2_add(i):
                    dve.wait_ge(p2_done[0], i + 1)
                    src = second_bank(0, i).rearrange("p (a k) -> p a k", k=NCH)
                    nc.vector.tensor_tensor(x_step(0, i), x_step(0, i), src, ALU.add).then_inc(x2_ready[0], 1)

                def fused_lo(e):
                    dve.wait_ge(fused_ready, e + 1)
                    nc.vector.tensor_tensor(out_p[1][:, e, :], fuse_bank(e)[:], out_p[0][:, e, :].bitcast(F32),
                                            ALU.subtract).then_inc(fused_lo_ready, 1)

                dve.wait_ge(gat_done, NB)
                dve.wait_ge(rstd1_ready, NB)
                dve.wait_ge(u_t_done, NB)
                for e in range(FUSED_FRONT):
                    dve.wait_ge(fused_done, e + 1)
                    nc.vector.tensor_copy(out_p[0][:, e, :], fuse_bank(e)[:]).then_inc(fused_ready, 1)
                    fused_lo(e)
                for lv in range(LEVELS):
                    ks_add(lv)
                for i in range(T):
                    p2_add(i)

                def scan_part(j, places):
                    for n in places:
                        for what, i in scan_work(j, n):
                            if what == "fuse":
                                fused_lo(i)

                def high_parts(j, places):
                    if DVE_ROUND <= j < NB:
                        for n in places:
                            half, c = divmod(n, HC)
                            m = 8 * j + n
                            dve.wait_ge(full_ready, m + 1 - 8 * DVE_ROUND)
                            dve.wait_ge(o_done, 2 * (j - 1) + half + 1)
                            nc.vector.tensor_copy(hid_p[0][:, half, c, :],
                                                  hid_f[:, m % HID_SLOTS, :]).then_inc(hid_ready, 1)
                            if n % 2 == 1:
                                dve.wait_ge(hid_ready, m + 1)
                                nc.vector.tensor_tensor(hid_p[1][:, half, c, :], hid_f[:, m % HID_SLOTS, :],
                                                        hid_p[0][:, half, c, :].bitcast(F32),
                                                        ALU.subtract).then_inc(hid_lo_dve, 1)

                for j in range(-3, NB + 1):
                    b = j + 1
                    if 0 <= b < NB:
                        dve.wait_ge(attn_done, b + 1)
                        dve.wait_ge(xp_ready, b + 1)
                        if b >= 1:
                            dve.wait_ge(xa_t_done, b)
                        for q in range(NQ):
                            s = slice(q * CH, (q + 1) * CH)
                            last = nc.vector.scalar_tensor_tensor(
                                out=xa[:, s], in0=bank[4][:, s], scalar=rstd2[:, b, 1, q:q + 1],
                                in1=xp[:, s], op0=ALU.mult, op1=ALU.add)
                        last.then_inc(xa_ready, 1)
                    if j < 0:
                        scan_part(j, [0])
                    b = j + 3
                    if b < NB:
                        for a in range(NP):
                            dve.wait_ge(xt_done, 2 * b + a + 1)
                            last = nc.vector.tensor_reduce(
                                amax[:, b % 2, :, 2 * a:2 * a + 2],
                                bank[a][:].rearrange("p (q n d) -> p q n d", q=NQ, n=2), AX.X, ALU.max,
                                apply_absolute_value=True)
                        last.then_inc(amax_ready, 1)
                        dve.wait_ge(amax_ready, b + 1)
                        chained(nc.vector.reciprocal(rcp[:, b % 2, :],
                                                     amax[:, b % 2, :, :].rearrange("p q n -> p (q n)")))
                        if b >= 2:
                            dve.wait_ge(rt_done, b - 1)
                        hi = r_s[:, b % 2, 0, :]
                        chained(nc.vector.tensor_scalar(hi.bitcast(F32R), rcp[:, b % 2, :], E2, None, ALU.mult))
                        nc.vector.scalar_tensor_tensor(out=r_s[:, b % 2, 1, :], in0=rcp[:, b % 2, :], scalar=E2,
                                                       in1=hi, op0=ALU.mult, op1=ALU.subtract).then_inc(rs_ready, 1)
                    if j < 0:
                        scan_part(j, [1])
                    high_parts(j, range(0, 2))
                    b = j + 1
                    if 0 <= b < NB:
                        dve.wait_ge(xaT_ready, b + 1)
                        if b >= 2:
                            dve.wait_ge(fc1_done, 8 * (b - 1))
                        for half in range(2):
                            view = "p (i k) -> p i k"
                            last = nc.vector.scalar_tensor_tensor(
                                out=xaT_p[1][:, b % 2, half, :].rearrange(view, i=T),
                                in0=bank[3][:].rearrange("p (i s k) -> p s i k", i=T, s=2)[:, half],
                                scalar=attn_c[:],
                                in1=xaT_p[0][:, b % 2, half, :].bitcast(F32).rearrange(view, i=T),
                                op0=ALU.add, op1=ALU.subtract)
                        last.then_inc(xaT_lo_ready, 1)
                    b = j + 2
                    if 0 <= b < NB:
                        dve.wait_ge(y_done, b + 1)
                        nc.vector.tensor_tensor(h[:, b, :], h[:, b, :], bank[2][:], ALU.add).then_inc(h2_ready, 1)
                        dve.wait_ge(h2_ready, b + 1)
                        statistics(b, st2, st2_ready, mv2, mv2_ready)
                        if b >= 2:
                            dve.wait_ge(rstd2_ready, b - 1)
                        dve.wait_ge(mv2_ready, b + 1)
                        v, t = mv2[:, b, :, 1], spread2[:, b % 2]
                        nc.vector.tensor_scalar(t[:, 0, :], v, EPS, None, ALU.add)
                        nc.vector.tensor_scalar(t[:, 1, :], v, 1.0 + EPS, EPS * EPS, ALU.mult,
                                                ALU.add).then_inc(v2_ready, 1)
                    if j < 0:
                        scan_part(j, [2])
                    high_parts(j, range(2, 4))
                    b = j + 3
                    if b < NB:
                        g, bb = divmod(b, GB)
                        if b == 0:
                            dve.wait_ge(fc1_split, NE)
                        for a in range(NP):
                            dve.wait_ge(R_done, 2 * b + a + 1)
                            if b >= 2:
                                dve.wait_ge(y_done, b - 1)
                            nc.vector.tensor_tensor(xh[:, b % 2, a, :],
                                                    X[:, g, a * GB + bb, :, :].rearrange("p i k -> p (i k)"),
                                                    bank[a][:], ALU.mult).then_inc(xh_ready, 1)
                    if j < 0:
                        scan_part(j, [3, 4, 5])
                    high_parts(j, range(4, 6))
                    if j >= 1:
                        o = j - 1
                        dve.wait_ge(gel_ready, o + 1)
                        dve.wait_ge(hT_ready, o + 1)
                        if o >= 2:
                            dve.wait_ge(stored[o % 2], 16 * (o // 2))
                        halves = [slice(0, 1), slice(1, 2)] if o == NB - 1 else [slice(0, 2)]
                        for n, s in enumerate(halves):
                            if n == 1:
                                dve.wait_ge(gel_ready, NB + 1)
                            view = "p (s i k) -> p s i k"
                            nc.vector.tensor_tensor(
                                res[:, o % 2, :].rearrange(view, s=2, i=T)[:, s],
                                gel[:, o % 2, :].rearrange(view, s=2, i=T)[:, s],
                                hT[:, o % HT_SLOTS, :].rearrange("p (i s k) -> p s i k", s=2, i=T)[:, s],
                                ALU.add).then_inc(res_ready, 1)
                    b = j + 2
                    if 0 <= b < NB:
                        dve.wait_ge(rstd2_ready, b + 1)
                        for q in range(NQ):
                            s = slice(q * CH, (q + 1) * CH)
                            last = nc.vector.tensor_scalar(xp[:, s], h[:, b, s], mv2[:, b, q, 0:1],
                                                           rstd2[:, b, 0, q:q + 1], ALU.subtract, ALU.mult)
                        last.then_inc(xp_ready, 1)
                    if j < 0:
                        scan_part(j, [6, 7])
                    high_parts(j, range(6, 8))

            @block.tensor
            def _(pe):
                mm = nc.tensor.matmul

                def prepare(t):
                    if t >= 2:
                        pe.wait_ge(prep_ready, t - 1)
                    dst = bank[4 + t % 2]
                    if t < N_POW:
                        out_, lhs, rhs, need = prep[t]
                        if need > max(t - 1, 0):
                            pe.wait_ge(prep_ready, need)
                        last = mm(dst[:, 0:out_.shape[1]], lhs, rhs, start=True, stop=True)
                    else:
                        pe.wait_ge(ld_pb, 16)
                        mm(dst[:, 0:1], pb[:, PB["attn"]], pa[:, PA["ln_b"]], start=True, stop=True)
                        mm(dst[:, 1:1 + NE], pb[:, PB["nw"]], pa[:, PA["fc2_b"]], start=True, stop=True)
                        pe.wait_ge(centre_ready, 1)
                        pe.wait_ge(attn_g_ready, 1)
                        last = mm(dst[:, P:P + CH], centre[:], attn_g[:], start=True, stop=True)
                    last.then_inc(prep_done, 1)

                def fuse_piece(e, c):
                    if c == 0:
                        if e == 0:
                            pe.wait_ge(ld_fc2, 16)
                            pe.wait_ge(ld_pb, 16)
                            pe.wait_ge(oh_ready, 2 * NB)
                        if e == FUSED_FRONT:
                            pe.wait_ge(x2_ready[0], T)
                            pe.wait_ge(rT_ready, 1)
                        if e >= 2:
                            pe.wait_ge(fused_lo_ready, e - 1)
                    last = mm(fuse_bank(e)[:, c * CH:(c + 1) * CH], fc2_w[:, e * HID + c * P:e * HID + (c + 1) * P],
                              pb[:, PB["nw"]], start=True, stop=True)
                    if c == HC - 1:
                        last.then_inc(fused_done, 1)

                def fuse(e):
                    for c in range(HC):
                        fuse_piece(e, c)

                def spread_ids(b):
                    for s in range(2):
                        n = 2 * b + s
                        if n >= 2:
                            pe.wait_ge(oh_ready, n - 1)
                        mm(bank[n % 2][:, 0:EXT * NCH // 2], rowsel[:, n, :], ids_b[:], start=True,
                           stop=True).then_inc(idb_done, 1)

                def gather(b):
                    pe.wait_ge(oh_ready, 2 * b + 2)
                    if b >= 1:
                        pe.wait_ge(h_ready, b)
                    for q in range(NQ):
                        for n, (tap, part) in enumerate([(0, 0), (0, 1), (1, 0), (1, 1)]):
                            at = (q * TQ + tap) * NCH
                            last = mm(bank[2][:, q * CH:(q + 1) * CH], onehot[:, b % 2, at:at + P], tab[:, part, tap, :],
                                      start=(n == 0), stop=(n == 3))
                    last.then_inc(gat_done, 1)

                def transpose_u(b):
                    pe.wait_ge(u_ready, b + 1)
                    pe.wait_ge(u_act_ready, sum(n < NQ for n in U_DVE[:b + 1]))
                    if b >= 1:
                        pe.wait_ge(uT_ready, b)
                    for q in range(NQ):
                        s = slice(q * CH, (q + 1) * CH)
                        last = nc.tensor.transpose(bank[3][:, s], u[:, b % 2, s], ident)
                    last.then_inc(u_t_done, 1)

                def scan_step(g, i):
                    if i == 0:
                        pe.wait_ge(uT_ready, GB * (g + 1))
                    w = GB * NCH
                    for a in range(NP):
                        if i >= 1:
                            pe.wait_ge(x_ready[g], NP * (i - 1) + a + 1)
                        elif g == 1:
                            pe.wait_ge(ends_ready[0], a + 1)
                        last = mm(bank[6 + a][:, 0:w], pa[:, PA["b"]][:, a * P:(a + 1) * P],
                                  uT[:, g * GB:(g + 1) * GB, i, :], start=True, stop=(i == 0))
                        if i >= 1:
                            last = mm(bank[6 + a][:, 0:w], a1, X[:, g, a * GB:(a + 1) * GB, i - 1, :],
                                      start=False, stop=True)
                        last.then_inc(step_done[g], 1)
                        if g == 0 and i in FUSE_STEPS:
                            fuse_piece(*divmod(FUSE_STEPS.index(i) * NP + a, HC))

                def ks_step(g, lv):
                    if lv == 0:
                        pe.wait_ge(init_ready, NG * NP)
                        pe.wait_ge(ends_ready[g], NP)
                        pe.wait_ge(prep_ready, N_POW)
                        pe.wait_ge(h_ready, NB)
                    else:
                        pe.wait_ge(ks_ready[g], lv)
                    mm(ks_bank(g, lv), step_of(lv), ks_src(g, lv), start=True, stop=True).then_inc(ks_done[g], 1)

                def second_pass(g, i):
                    if i == 0:
                        pe.wait_ge(ks_ready[g], LEVELS)
                        pe.wait_ge(prep_ready, N_PREP)
                        pe.wait_ge(fused_lo_ready, FUSED_FRONT)
                        pe.wait_ge(ends_ready[g], NP)
                    if i >= len(P2_BANKS[g]):
                        pe.wait_ge((x2_ready[0], corr_ready)[g], i + 1 - len(P2_BANKS[g]))
                    mm(second_bank(g, i), a1 if i == 0 else pw[:, i + 1, :],
                       E[:, g, :, :].rearrange("p a k -> p (a k)"), start=True, stop=True).then_inc(p2_done[g], 1)

                pe.wait_ge(ld_pc, 16)
                pe.wait_ge(amax_e_ready, 1)
                nc.tensor.transpose(bank[6][0:1, 0:VOC], amax_e[:], ident[0:VOC, 0:VOC]).then_inc(amax_t_done, 1)
                pe.wait_ge(pool_const, 2)
                pe.wait_ge(amax_row_ready, 1)
                mm(bank[7][:, 0:1], ones1[:], amax_row[:], start=True, stop=True).then_inc(amax_bc_done, 1)
                pe.wait_ge(ids_ready, 1)
                spread_ids(0)
                spread_ids(1)
                pe.wait_ge(ld_pa, 32)
                for b in range(NB + 2):
                    if b == 0:
                        pe.wait_ge(tab_ready, 1)
                    if b < NB:
                        gather(b)
                    if b + 2 < NB:
                        spread_ids(b + 2)
                    for t in prep_tasks(b, 0):
                        prepare(t)
                    if b >= 2:
                        transpose_u(b - 2)
                    for t in prep_tasks(b, 1):
                        prepare(t)
                    for i in embed_round_steps(b):
                        scan_step(0, i)
                prepare(N_PREP - 1)
                for lv in range(LEVELS):
                    ks_step(0, lv)
                    scan_step(1, lv)
                for i in range(T):
                    second_pass(0, i)
                    if (i + 1) % (T // WITH_SECOND) == 0:
                        scan_step(1, LEVELS + i // (T // WITH_SECOND))

                def transpose_x(b):
                    g, bb = divmod(b, GB)
                    pe.wait_ge(x2_ready[g], T)
                    for a in range(NP):
                        if b >= 1:
                            pe.wait_ge(xh_ready, 2 * (b - 1) + a + 1)
                        for q in range(NQ):
                            last = nc.tensor.transpose(bank[a][:, q * P:(q + 1) * P],
                                                       X[:, g, a * GB + bb, q * TQ:(q + 1) * TQ, :].rearrange("p i k -> p (i k)"),
                                                       ident)
                        last.then_inc(xt_done, 1)

                def transpose_r(b):
                    pe.wait_ge(rs_ready, b + 1)
                    if b == 0:
                        pe.wait_ge(x2_ready[0], T)
                    elif b == 1:
                        pe.wait_ge(fused_lo_ready, NE - 1)
                    else:
                        pe.wait_ge(xa_ready, b - 1)
                    nc.tensor.transpose(bank_rt, r_s[:, b % 2, :, :].rearrange("p s n -> p (s n)"),
                                        ident).then_inc(rt_done, 1)

                def spread_r(b):
                    pe.wait_ge(rT_ready, b + 1)
                    pe.wait_ge(sel_ready, 1)
                    pe.wait_ge(amax_ready, b + 1)
                    for a in range(NP):
                        mm(bank[a][:], sel_r[:, a * P:(a + 1) * P], r_T[:, b % 2, :], start=True,
                           stop=True).then_inc(R_done, 1)

                def mixer_out(b, q):
                    if q == 0:
                        pe.wait_ge(xh_ready, 2 * b + 2)
                        pe.wait_ge(ks_ready[0], LEVELS)
                        if b >= 1:
                            pe.wait_ge(h2_ready, b)
                    dst = bank[2][:, q * CH:(q + 1) * CH]
                    mm(dst, uT[:, b, q * TQ:(q + 1) * TQ, :].rearrange("p i k -> p (i k)"), pb[:, PB["d"]],
                       start=True, stop=False)
                    for a in range(NP):
                        last = mm(dst, xh[:, b % 2, a, q * P:(q + 1) * P], pb[:, PB["c"]][:, a * CH:(a + 1) * CH],
                                  start=False, stop=(a == NP - 1))
                    if q == NQ - 1:
                        last.then_inc(y_done, 1)

                def transpose_h(b):
                    pe.wait_ge(h2_ready, b + 1)
                    pe.wait_ge(rT_ready, min(b + 2, NB))
                    if b == NB - 1:
                        pe.wait_ge(xa_ready, b)
                    for q in range(NQ):
                        s = slice(q * CH, (q + 1) * CH)
                        last = nc.tensor.transpose(bank[4][:, s], h[:, b, s], ident)
                    last.then_inc(h_t_done, 1)

                def attn(b):
                    pe.wait_ge(hT_ready, b + 1)
                    for q in range(NQ):
                        s = slice(q * CH, (q + 1) * CH)
                        last = mm(bank[4][:, s], hT[:, b % HT_SLOTS, s], attn_m[:], start=True, stop=True)
                    last.then_inc(attn_done, 1)

                def transpose_xa(b):
                    pe.wait_ge(xa_ready, b + 1)
                    if b == 0:
                        pe.wait_ge(uT_ready, NB)
                    else:
                        pe.wait_ge(xaT_lo_ready, b)
                    for q in range(NQ):
                        s = slice(q * CH, (q + 1) * CH)
                        last = nc.tensor.transpose(bank[3][:, s], xa[:, s], ident)
                    last.then_inc(xa_t_done, 1)

                def fc1_part(b, n):
                    half, c = divmod(n, HC)
                    e = expert(b, half)
                    if n == 0:
                        pe.wait_ge(xaT_ready, b + 1)
                        if b == 0:
                            pe.wait_ge(fc1_split, NE)
                            pe.wait_ge(corr_ready, T)
                            pe.wait_ge(fused_lo_ready, NE)
                    before = 8 * b + n - 2
                    if before >= 8 * DVE_ROUND:
                        pe.wait_ge(full_ready, before + 1 - 8 * DVE_ROUND)
                    elif before >= 0:
                        pe.wait_ge(hid_ready, before + 1)
                    for k, (w, m) in enumerate(PARTS):
                        if n == 0 and m == 1:
                            pe.wait_ge(xaT_lo_ready, b + 1)
                        last = mm(bank[5 + n % 2][:, 0:HALF], fc1_p[w][:, e * HID + c * P:e * HID + (c + 1) * P],
                                  xaT_p[m][:, b % 2, half, :], start=(k == 0), stop=(k == len(PARTS) - 1))
                    last.then_inc(fc1_done, 1)

                def out_part(part):
                    b, n = divmod(part, 8)
                    half, c = divmod(n, HC)
                    e = expert(b, half)
                    if n == 0:
                        if b == NB - 3:
                            pe.wait_ge(xh_ready, NP * NB)
                        if b >= NB - 3:
                            pe.wait_ge(gel_ready, b - 1)
                        elif b >= 1:
                            pe.wait_ge(gel_ready, b)
                    pe.wait_ge(hid_ready, part + 1)
                    for k, (w, m) in enumerate(PARTS):
                        if m == 1:
                            wait_low(pe, part)
                        last = mm(out_bank(b, half)[:, half * HALF:(half + 1) * HALF], out_p[w][:, e, c * CH:(c + 1) * CH],
                                  hid_p[m][:, half, c, :], start=(c == 0 and k == 0),
                                  stop=(c == HC - 1 and k == len(PARTS) - 1))
                    if c == HC - 1:
                        last.then_inc(o_done, 1)

                def fill(j, n):
                    if j < 0:
                        for what, i in scan_work(j, n):
                            if what == "fuse":
                                fuse(i)
                            else:
                                {"step": scan_step, "doubling": ks_step, "second": second_pass}[what](1, i)
                    else:
                        if n == LAG - 1 and j >= 1:
                            out_part(8 * j + n - LAG)
                        fc1_part(j, n)
                        if n != LAG - 1 and 8 * j + n >= LAG:
                            out_part(8 * j + n - LAG)

                for j in range(-3, NB):
                    scaled, mixed, attended = j + 3, j + 2, j + 1
                    if scaled < NB:
                        transpose_x(scaled)
                    fill(j, 0)
                    fill(j, 1)
                    if 0 <= mixed < NB:
                        mixer_out(mixed, 0)
                        mixer_out(mixed, 1)
                    fill(j, 2)
                    if scaled < NB:
                        transpose_r(scaled)
                    if 0 <= mixed < NB:
                        mixer_out(mixed, 2)
                    if 0 <= attended < NB:
                        transpose_xa(attended)
                    fill(j, 3)
                    if 0 <= mixed < NB:
                        mixer_out(mixed, 3)
                    if scaled < NB:
                        spread_r(scaled)
                    fill(j, 4)
                    fill(j, 5)
                    if 0 <= mixed < NB:
                        transpose_h(mixed)
                    fill(j, 6)
                    fill(j, 7)
                    if 0 <= mixed < NB:
                        attn(mixed)
                for part in range(8 * NB - LAG, 8 * NB):
                    out_part(part)

def kernel(x, L0_tok_emb_weight, L0_tok_conv_weight, L0_attn_init_states, L0_attn_A, L0_attn_B, L0_attn_C,
           L0_attn_D, L0_ffn_ln_g, L0_ffn_ln_b, L0_ffn_attn_w, L0_ffn_attn_b, L0_ffn_gate_w, L0_ffn_fc1_w,
           L0_ffn_fc1_b, L0_ffn_fc2_w, L0_ffn_fc2_b, L0_ffn_next_w, L0_ffn_next_b):
    import concourse.bacc as bacc
    from concourse.bass_utils import run_bass_kernel_spmd
    import ml_dtypes

    f = lambda a: np.asarray(a)
    ids = f(x).reshape(NB, NCH, T).transpose(0, 2, 1)
    before = np.full((NB, 1, NCH), -1, ids.dtype)
    before[:, 0, 1:] = ids[:, T - 1, :-1]
    ids = np.concatenate([before, ids], 1).reshape(2 * NB, EXT * NCH // 2)

    def diag(a):
        out = np.zeros((P, P), a.dtype)
        out[:DH, :DH] = a
        out[DH:, DH:] = a
        return out

    A = f(L0_attn_A)
    parts = dict(
        a=diag(A), at=diag(A.T), b=f(L0_attn_B),
        init=f(L0_attn_init_states).reshape(NP, P).T, ln_g=f(L0_ffn_ln_g)[:, None], ln_b=f(L0_ffn_ln_b)[:, None],
        attn_b=f(L0_ffn_attn_b)[:, None], next_b=f(L0_ffn_next_b)[:, None],
        fc1_b=f(L0_ffn_fc1_b).reshape(NE * HC, P).T, fc2_b=f(L0_ffn_fc2_b).T)
    pack_a = np.concatenate([parts[n] for n in PA_COLS], 1)
    parts = dict(nw=f(L0_ffn_next_w).T, c=f(L0_attn_C).reshape(NP, P, CH).transpose(1, 0, 2).reshape(P, NP * CH),
                 d=f(L0_attn_D), attn=f(L0_ffn_attn_w).T)
    pack_b = np.concatenate([parts[n] for n in PB_COLS], 1)
    tile = np.zeros((P, NQ), np.float32)
    rows = tile[:NS * NQ * NH].reshape(NS, NQ, NH, NQ)
    sel = np.zeros((NS, NQ, NH, NP, 2, DH), np.float32)
    for q in range(NQ):
        rows[:, q, :, q] = 1
    for n in range(NH):
        sel[:, :, n, n // 2, n % 2, :] = 1
    pack_c = np.concatenate([np.eye(P, dtype=np.float32), np.arange(P, dtype=np.float32)[:, None], tile], 1)
    arrays = dict(
        ids=ids, emb=f(L0_tok_emb_weight), conv=f(L0_tok_conv_weight)[:, 0, :].T.reshape(1, 2 * CH),
        pack_a=pack_a, pack_b=pack_b, sel=sel.reshape(NS * NQ * NH, NP * P),
        pack_c=pack_c, rows=np.repeat(np.eye(2 * NB, dtype=ml_dtypes.bfloat16), P, 1),
        fc1=f(L0_ffn_fc1_w).transpose(2, 0, 1).reshape(P, NE * HID),
        fc2=f(L0_ffn_fc2_w).transpose(1, 0, 2))
    arrays = {n: np.ascontiguousarray(a) for n, a in arrays.items()}
    nc = bacc.Bacc("TRN2", target_bir_lowering=False, num_devices=1)
    args = {n: nc.dram_tensor(f"in_{n}", a.shape, mybir.dt.from_np(a.dtype), kind="ExternalInput").ap()
            for n, a in arrays.items()}
    out = nc.dram_tensor("out", (NB, P, L), F32, kind="ExternalOutput").ap()
    build(nc, out=out, **args)
    r = run_bass_kernel_spmd(nc, [{f"in_{n}": a for n, a in arrays.items()}], core_ids=[0])
    got = r.results[0]["out"].reshape(NB, CH, 2, T, NCH // 2)
    return np.ascontiguousarray(got.transpose(0, 2, 4, 3, 1)).reshape(NB, L, CH)
```
